# Optimizing a Trainium2 kernel written in Bass

```python
import numpy as np
import jax
import jax.numpy as jnp

def _softmax(x, axis=-1):
    return jax.nn.softmax(x, axis=axis)

def _gelu(x):
    return jax.nn.gelu(x, approximate=True)

def _silu(x):
    return jax.nn.silu(x)

def _sigmoid(x):
    return jax.nn.sigmoid(x)

def _layernorm(x, axis=-1, eps=1e-05):
    m = jnp.mean(x, axis=axis, keepdims=True)
    v = jnp.var(x, axis=axis, keepdims=True)
    return (x - m) / jnp.sqrt(v + eps)

def _scatter_add(tgt, idx, src, axis=0):
    return tgt.at[idx].add(src)

def _segment_sum(src, seg, n):
    return jax.ops.segment_sum(src, seg, n)
kernel_name = 'mk_adaln_d1_jaxref_r4_aad4ed'

def setup_inputs(seed: int=0):
    np.random.seed(seed)
    _w = jnp.asarray

    def _L0_attn_setup():
        import jax, jax.numpy as jnp
        import numpy as np
        HEADS = 16

        def fenwick_mask(T):
            m = np.zeros((T, T), dtype=bool)
            for i in range(T):
                j = i + 1
                while j <= T:
                    m[i, j - 1] = True
                    j += j & -j
                step = 1
                while i - step >= 0:
                    m[i, i - step] = True
                    step *= 2
            m &= np.tril(np.ones((T, T), dtype=bool))
            return jnp.asarray(m)
        key = jax.random.key(seed)
        ks = jax.random.split(key, 4)
        B, T, C = (2, 512, 256)
        x = jax.random.normal(ks[0], (B, T, C), dtype=jnp.float32)
        W_qkv = jax.random.normal(ks[1], (C, 3 * C), dtype=jnp.float32) * C ** (-0.5)
        b_qkv = jnp.zeros((3 * C,), dtype=jnp.float32)
        W_proj = jax.random.normal(ks[2], (C, C), dtype=jnp.float32) * C ** (-0.5)
        b_proj = jnp.zeros((C,), dtype=jnp.float32)
        return {'x': x, 'W_qkv': W_qkv, 'b_qkv': b_qkv, 'W_proj': W_proj, 'b_proj': b_proj}
    _L0_attn_in = _L0_attn_setup()

    def _L0_ffn_setup():
        import jax, jax.numpy as jnp
        import numpy as np
        B, S, D = (8, 1024, 256)
        E, R, K = (6, 16, 2)
        key = jax.random.key(seed)
        ks = jax.random.split(key, 9)
        sc = 0.02
        return {'x': jax.random.normal(ks[0], (B, S, D), jnp.float32), 'base_W': jax.random.normal(ks[1], (D, D), jnp.float32) * sc, 'base_b': jax.random.normal(ks[2], (D,), jnp.float32) * sc, 'shared_A': jax.random.normal(ks[3], (R, D), jnp.float32) * sc, 'shared_B': jax.random.normal(ks[4], (D, R), jnp.float32) * sc, 'routed_A': jax.random.normal(ks[5], (E, R, D), jnp.float32) * sc, 'routed_B': jax.random.normal(ks[6], (E, D, R), jnp.float32) * sc, 'router_W': jax.random.normal(ks[7], (E, D), jnp.float32) * sc, 'router_b': jax.random.normal(ks[8], (E,), jnp.float32) * sc}
    _L0_ffn_in = _L0_ffn_setup()
    _L0_c = _w((lambda *s: np.random.randn(*s).astype(np.float32) * 0.05)(2, 256))
    _L0_wmod = _w((lambda *s: np.random.randn(*s).astype(np.float32) * 0.05)(256, 6 * 256) * 256 ** (-0.5))
    _d = {'L0_attn_x': _L0_attn_in['x'], 'L0_attn_W_qkv': _L0_attn_in['W_qkv'], 'L0_attn_b_qkv': _L0_attn_in['b_qkv'], 'L0_attn_W_proj': _L0_attn_in['W_proj'], 'L0_attn_b_proj': _L0_attn_in['b_proj'], 'L0_ffn_base_W': _L0_ffn_in['base_W'], 'L0_ffn_base_b': _L0_ffn_in['base_b'], 'L0_ffn_shared_A': _L0_ffn_in['shared_A'], 'L0_ffn_shared_B': _L0_ffn_in['shared_B'], 'L0_ffn_routed_A': _L0_ffn_in['routed_A'], 'L0_ffn_routed_B': _L0_ffn_in['routed_B'], 'L0_ffn_router_W': _L0_ffn_in['router_W'], 'L0_ffn_router_b': _L0_ffn_in['router_b'], 'L0_c': _L0_c, 'L0_wmod': _L0_wmod}
    _x0 = _d['L0_attn_x']
    _d['L0_attn_x'] = jax.random.normal(jax.random.fold_in(jax.random.key(seed), 1), (2, 2048, 256), dtype=_x0.dtype)
    del _x0
    return _d

def reference(L0_attn_x, L0_attn_W_qkv, L0_attn_b_qkv, L0_attn_W_proj, L0_attn_b_proj, L0_ffn_base_W, L0_ffn_base_b, L0_ffn_shared_A, L0_ffn_shared_B, L0_ffn_routed_A, L0_ffn_routed_B, L0_ffn_router_W, L0_ffn_router_b, L0_c, L0_wmod):

    def _L0_attn_ref(x, W_qkv, b_qkv, W_proj, b_proj):
        import jax, jax.numpy as jnp
        import numpy as np
        HEADS = 16

        def fenwick_mask(T):
            m = np.zeros((T, T), dtype=bool)
            for i in range(T):
                j = i + 1
                while j <= T:
                    m[i, j - 1] = True
                    j += j & -j
                step = 1
                while i - step >= 0:
                    m[i, i - step] = True
                    step *= 2
            m &= np.tril(np.ones((T, T), dtype=bool))
            return jnp.asarray(m)
        B, T, C = x.shape
        H = HEADS
        Dh = C // H
        scale = Dh ** (-0.5)
        qkv = (x @ W_qkv + b_qkv).reshape(B, T, 3, H, Dh)
        qkv = jnp.transpose(qkv, (2, 0, 3, 1, 4))
        q, k, v = (qkv[0], qkv[1], qkv[2])
        attn = jnp.einsum('bhtd,bhsd->bhts', q, k) * scale
        mask = fenwick_mask(T)
        attn = jnp.where(mask[None, None], attn, -jnp.inf)
        attn = jax.nn.softmax(attn, axis=-1)
        out = jnp.einsum('bhts,bhsd->bhtd', attn, v)
        out = jnp.transpose(out, (0, 2, 1, 3)).reshape(B, T, C)
        return out @ W_proj + b_proj

    def _L0_ffn_ref(x, base_W, base_b, shared_A, shared_B, routed_A, routed_B, router_W, router_b):
        import jax, jax.numpy as jnp
        import numpy as np
        B, S, D = (8, 1024, 256)
        E, R, K = (6, 16, 2)
        base_out = jax.lax.stop_gradient(jnp.einsum('bsi,oi->bso', x, base_W) + base_b)
        shared_out = jnp.einsum('bsr,or->bso', jnp.einsum('bsi,ri->bsr', x, shared_A), shared_B)
        logits = jnp.einsum('bsi,ei->bse', x, router_W) + router_b
        gate = jax.nn.softmax(logits, axis=-1)
        topk_w, topk_i = jax.lax.top_k(gate, K)
        sparse_w = jnp.sum(jax.nn.one_hot(topk_i, E, dtype=gate.dtype) * topk_w[..., None], axis=-2)
        sparse_w = sparse_w / (jnp.sum(sparse_w, axis=-1, keepdims=True) + 1e-06)
        h = jnp.einsum('bsi,eri->bser', x, routed_A)
        routed_outs = jnp.einsum('bser,eor->bseo', h, routed_B)
        routed_out = jnp.einsum('bseo,bse->bso', routed_outs, sparse_w)
        return base_out + shared_out + routed_out
    x = L0_attn_x
    mod = (_silu(L0_c) @ L0_wmod).reshape(L0_c.shape[0], 6, 1, -1)
    sa, ca, ga, sb, cb, gb = (mod[:, 0], mod[:, 1], mod[:, 2], mod[:, 3], mod[:, 4], mod[:, 5])
    ga = (2 * (ga >= 0) - 1) * jnp.maximum(jnp.abs(ga), 0.25)
    gb = (2 * (gb >= 0) - 1) * jnp.maximum(jnp.abs(gb), 0.25)
    h = _layernorm(x, axis=-1) * (1 + ca) + sa
    x = x + ga * _L0_attn_ref(h, L0_attn_W_qkv, L0_attn_b_qkv, L0_attn_W_proj, L0_attn_b_proj)
    h = _layernorm(x, axis=-1) * (1 + cb) + sb
    x = x + gb * _L0_ffn_ref(h, L0_ffn_base_W, L0_ffn_base_b, L0_ffn_shared_A, L0_ffn_shared_B, L0_ffn_routed_A, L0_ffn_routed_B, L0_ffn_router_W, L0_ffn_router_b)
    return x

_drawn_inputs = setup_inputs


def setup_inputs(seed=0):
    import zlib

    import numpy as np

    out = dict(_drawn_inputs(seed))
    spreads = {'L0_attn_b_qkv': (0.0, 0.313), 'L0_attn_b_proj': (0.0, 0.304)}
    factors = {'L0_ffn_base_b': 8.0,
     'L0_ffn_shared_A': 8.0,
     'L0_ffn_shared_B': 8.0,
     'L0_ffn_routed_A': 8.0,
     'L0_ffn_routed_B': 8.0,
     'L0_ffn_router_W': 8.0,
     'L0_ffn_router_b': 8.0}
    for name, (base, spread) in spreads.items():
        noise = np.random.default_rng([zlib.crc32(name.encode()), seed]).standard_normal(out[name].shape)
        drawn = base * np.exp(spread * noise) if base else spread * noise
        out[name] = jnp.asarray(drawn.astype(out[name].dtype))
    for name, factor in factors.items():
        out[name] = (out[name] * factor).astype(out[name].dtype)
    return out
```

```python
from contextlib import ExitStack

import concourse.bass as bass
from concourse import mybir

F32 = mybir.dt.float32
BF16 = mybir.dt.bfloat16
ALU = mybir.AluOpType
ACT = mybir.ActivationFunctionType
AX = mybir.AxisListType

P = 128
BATCH, SEQ, D = 2, 2048, 256
HEADS, DH = 16, 16
HALVES = D // P
HH = HEADS // HALVES
TILES = SEQ // P
CT = 4
CHUNKS = TILES // CT
CW = CT * P
UNITS = BATCH * CHUNKS
PRE = 8
E, R, TOPK = 6, 16, 2
NR = E * R
NG = NR + R
NA = NG + E
SCALE = DH ** -0.5
EPS = 1e-5
MASKED = -1e30

DIST = [0, 16, 32, 64, 128, 256, 512, 1024, 1, 2, 4, 8]
ND = len(DIST)
SHIFT = [d // 16 for d in DIST]
BACK = [d if d < 16 else 0 for d in DIST]
COLS = [d * P if d < 16 else d // 16 for d in DIST]
PERMS = [0, 1, 2, 4, 8, 16, 32, 64]
NSH = 7

QK_ROUNDS = [[("v", r), ("v", 4 + r), ("p", 8 + r)] for r in range(4)]
PV_ORDER = [("v", 0), ("p", 8), ("v", 1), ("v", 2), ("p", 9), ("v", 3), ("v", 4), ("p", 10), ("v", 5),
            ("v", 6), ("p", 11), ("v", 7)]
QK_V = [k for r in QK_ROUNDS for e, k in r if e == "v"]
QK_P = [k for r in QK_ROUNDS for e, k in r if e == "p"]
PV_V = [k for e, k in PV_ORDER if e == "v"]
PV_P = [k for e, k in PV_ORDER if e == "p"]
NV, NP = len(QK_V) + len(PV_V), len(QK_P) + len(PV_P)
VSLOTS, PSLOTS = 4, 2
assert NV % VSLOTS == 0 and NP % PSLOTS == 0

VA_STEPS, VB_STEPS, VC_STEPS = 7, 4, 20
PA_STEPS, PC_STEPS = 3, 3


def ds(start, size):
    return bass.ds(start, size)


def build(nc, x, cT, wmod, wqkv, bqkv, wproj, bproj, wbase, wdown, wup, rb, perm, permT, sel, mask, maskrow,
          lower, out):
    x_v = x.rearrange("b (p j) c -> b p j c", j=TILES)
    out_v = out.rearrange("b (p j) c -> b p j c", j=TILES)

    with ExitStack() as ctx:
        def sb(name, shape, dt=F32):
            return ctx.enter_context(nc.sbuf_tensor(name, shape, dt))

        def bank(name):
            return ctx.enter_context(nc.psum_tensor(name, [P, 512], F32))

        def sem(name):
            return ctx.enter_context(nc.semaphore(name))

        KW = (PRE + TILES) * P
        keysT = [sb(f"keysT{b}", [P, HALVES, KW]) for b in range(BATCH)]
        vals = [sb(f"vals{b}", [P, (PRE + TILES) * D]) for b in range(BATCH)]
        queriesT = sb("queriesT", [P, HALVES, SEQ])
        vring = [sb(f"vprod{s}", [P, 2 * CW]) for s in range(VSLOTS)]
        pring = [sb(f"pprod{s}", [P, 2 * CW]) for s in range(PSLOTS)]
        xa = sb("xa", [P, CT, D])
        xb = sb("xb", [P, CT, D])
        xhatA = sb("xhatA", [P, CT, D])
        hT = sb("hT", [P, HALVES, CW])
        x2 = sb("x2", [P, CT, D])
        xhatC = x2
        h2T = sb("h2T", [P, HALVES, CW])
        probs = sb("probs", [P, ND, CT * HEADS])
        attnT = sb("attnT", [P, HALVES, CW])
        scoresT = attnT[0:ND * HH, :, :]
        smax = sb("smax", [P, CT * HEADS])
        ssum = sb("ssum", [P, CT * HEADS])
        srec = sb("srec", [P, CT * HEADS])
        bnA = sb("bnA", [P, CT, 6])
        mvA = sb("mvA", [P, 5, CT])
        bnC = sb("bnC", [P, CT, 6])
        mvC = sb("mvC", [P, 5, CT])
        veA = sb("veA", [P, 3, CT])
        veC = sb("veC", [P, 3, CT])
        rstdA = sb("rstdA", [P, CT])
        rstdC = sb("rstdC", [P, CT])
        biasA = sb("biasA", [P, CT])
        biasC = sb("biasC", [P, CT])
        lnc = sb("lnc", [P, 4, CT])
        lg = sb("lg", [P, CT, E])
        lmax = sb("lmax", [P, CT])
        lsub = sb("lsub", [P, CT, E])
        lexp = sb("lexp", [P, CT, E])
        above = sb("above", [P, CT, E, E])
        level = sb("level", [P, CT, E, E])
        rank = sb("rank", [P, CT, E])
        picked = sb("picked", [P, CT, E])
        zall = sb("zall", [P, CT])
        zpick = sb("zpick", [P, CT])
        zrec = sb("zrec", [P, CT])
        wsel = sb("wsel", [P, CT, E])
        lora = sb("lora", [P, CT, NG + 1])
        loraT = sb("loraT", [NG + 1, CW])
        wqkv_sb = sb("wqkv_sb", [P, HALVES, 3 * D])
        bqkv_sb = sb("bqkv_sb", [P, 3 * HALVES])
        wdown_sb = sb("wdown_sb", [P, HALVES, NA])
        wproj_s = [sb(f"wproj_s{b}", [P, HALVES, D]) for b in range(BATCH)]
        wbase_s = [sb(f"wbase_s{b}", [P, HALVES, D]) for b in range(BATCH)]
        wup_s = [sb(f"wup_s{b}", [NG + 1, D]) for b in range(BATCH)]
        brow = [sb(f"brow{b}", [P, D]) for b in range(BATCH)]
        rb_sb = sb("rb_sb", [P, E])
        lower_sb = sb("lower_sb", [P, E, E])
        perm_sb = sb("perm_sb", [P, len(PERMS), P])
        permT_sb = sb("permT_sb", [P, NSH, P])
        sel_sb = sb("sel_sb", [P, 4, 32])
        mask_sb = sb("mask_sb", [ND, SEQ], BF16)
        maskrow_sb = sb("maskrow_sb", [ND, ND * HH], BF16)
        cT_sb = sb("cT_sb", [P, HALVES, BATCH])
        silu = sb("silu", [P, 3, HALVES, BATCH])
        modT = sb("modT", [P, 4, HALVES, BATCH])
        room = vals[1]
        wmod_sb = room[:, 0:2 * 6 * D].rearrange("p (k n) -> p k n", k=HALVES)
        at = 2 * 6 * D
        wproj_sb = room[:, at:at + 2 * D].rearrange("p (k n) -> p k n", k=HALVES)
        at += 2 * D
        wbase_sb = room[:, at:at + 2 * D].rearrange("p (k n) -> p k n", k=HALVES)
        at += 2 * D
        wup_sb = room[0:NG + 1, at:at + D]
        at += D
        bproj_sb = room[:, at:at + D]
        at += D
        gates = room[:, at:at + 4 * D].rearrange("p (b v n) -> p b v n", b=BATCH, v=2)
        gsign = vring[0][:, :].rearrange("p (b v n) -> p b v n", b=BATCH, v=2)
        silub = vring[1][:, 0:4 * P].rearrange("p (k b n) -> p k b n", k=HALVES, b=BATCH)

        pS = [bank("pS0"), bank("pS1")]
        pO = [bank("pO0"), bank("pO1")]
        pB = [bank("pB0"), bank("pB1")]
        pA = [bank("pA0"), bank("pA1")]

        ld_mod, ld_x, ld_qkv, ld_const, ld_scaled = (sem(n) for n in
                                                      ("ld_mod", "ld_x", "ld_qkv", "ld_const", "ld_scaled"))
        xa_in, xb_in, out_done = sem("xa_in"), sem("xb_in"), sem("out_done")
        expc_done, silu_done, mod_full, modT_done, gates_done, scaled_done = (
            sem(n) for n in ("expc_done", "silu_done", "mod_full", "modT_done", "gates_done", "scaled_done"))
        const_done, setup_v = sem("const_done"), sem("setup_v")
        statsA, rstdA_done, xhatA_done = sem("statsA"), sem("rstdA_done"), sem("xhatA_done")
        statsC, rstdC_done, xhatC_done = sem("statsC"), sem("rstdC_done"), sem("xhatC_done")
        a_full, a_read, kpre_done = sem("a_full"), sem("a_read"), sem("kpre_done")
        vprod_done, pprod_done = sem("vprod_done"), sem("pprod_done")
        vprod_used, pprod_used = sem("vprod_used"), sem("pprod_used")
        sT_read = sem("sT_read")
        stok_full, ssub_done, exp_done, probs_done = (sem(n) for n in
                                                      ("stok_full", "ssub_done", "exp_done", "probs_done"))
        pshift_full, attnT_read = sem("pshift_full"), sem("attnT_read")
        xb_pre, y_full, y_read = sem("xb_pre"), sem("y_full"), sem("y_read")
        h2T_full, h2T_read = sem("h2T_full"), sem("h2T_read")
        down_full, lsub_done, lexp_done, lora_done = (sem(n) for n in
                                                      ("down_full", "lsub_done", "lexp_done", "lora_done"))
        loraT_full, loraT_read, y2_full, y2_read = (sem(n) for n in
                                                    ("loraT_full", "loraT_read", "y2_full", "y2_read"))
        va_step, vb_step, vc_step, pa_step, pc_step = (sem(n) for n in
                                                       ("va_step", "vb_step", "vc_step", "pa_step", "pc_step"))

        def need(eng, s, value):
            if not isinstance(value, int) or value > 0:
                eng.wait_ge(s, value)

        def steps(eng, s, base):
            count = [0]

            def link(ins):
                count[0] += 1
                ins.then_inc(s, 1)
                eng.wait_ge(s, base + count[0])
            return link, count

        def a_base(u, b):
            return 8 * u + 4 * b

        def values_there(b):
            return a_base(CHUNKS * (b + 1), b) + 4

        block = ctx.enter_context(nc.Block())

        @block.sync
        def _(sp):
            def chunk_of(t, u):
                return t[u // CHUNKS, :, CT * (u % CHUNKS):CT * (u % CHUNKS) + CT, :]

            def load_xa(u):
                need(sp, xhatA_done, u)
                sp.dma_start(xa[:, :, :], chunk_of(x_v, u)).then_inc(xa_in, 16)

            def load_xb(u):
                need(sp, y2_read, 2 * u)
                sp.dma_start(xb[:, :, :], chunk_of(x_v, u)).then_inc(xb_in, 16)

            def store(u):
                sp.wait_ge(y2_read, 2 * u + 2)
                sp.dma_start(chunk_of(out_v, u), x2[:, :, :]).then_inc(out_done, 16)

            load_xa(0)
            for dst, src in ((cT_sb[:, :, :], cT), (wmod_sb, wmod.rearrange("(k p) n -> p k n", p=P))):
                sp.dma_start(dst, src).then_inc(ld_mod, 16)
            for dst, src in ((wqkv_sb[:, :, :], wqkv.rearrange("(k p) n -> p k n", p=P)), (bqkv_sb[:, :], bqkv),
                             (perm_sb[:, :, :], perm)):
                sp.dma_start(dst, src).then_inc(ld_qkv, 16)
            for dst, src in ((wproj_sb, wproj.rearrange("(k p) n -> p k n", p=P)),
                             (wbase_sb, wbase.rearrange("(k p) n -> p k n", p=P)), (wup_sb, wup),
                             (bproj_sb, bproj.rearrange("(a n) -> a n", a=1).broadcast_to([P, D]))):
                sp.dma_start(dst, src).then_inc(ld_scaled, 16)
            for dst, src in ((permT_sb[:, :, :], permT), (sel_sb[:, :, :], sel), (mask_sb[:, :], mask),
                             (maskrow_sb[:, :], maskrow),
                             (wdown_sb[:, :, :], wdown.rearrange("(k p) n -> p k n", p=P)),
                             (rb_sb[:, :], rb.rearrange("(a n) -> a n", a=1).broadcast_to([P, E])),
                             (lower_sb[:, :, :], lower)):
                sp.dma_start(dst, src).then_inc(ld_const, 16)
            for u in range(1, CHUNKS):
                load_xa(u)
            for u in range(UNITS):
                if u + CHUNKS < UNITS:
                    load_xa(u + CHUNKS)
                if u:
                    store(u - 1)
                load_xb(u)
            store(UNITS - 1)
            sp.wait_ge(out_done, 16 * UNITS)

        @block.gpsimd
        def _(pool):
            g = nc.gpsimd

            def setup():
                for n, value in enumerate((D * EPS, -0.5, D ** 0.5, -0.5 * D ** 0.5)):
                    g.memset(lnc[:, n, :], value).then_inc(const_done, 1)
                g.memset(lora[:, :, NG:NG + 1], 1.0).then_inc(const_done, 1)
                pool.wait_ge(const_done, 5)

            def scale_weights():
                pool.wait_ge(gates_done, 1)
                pool.wait_ge(ld_scaled, 64)
                for b in range(BATCH):
                    for k in range(HALVES):
                        g.tensor_tensor(wproj_s[b][:, k, :], wproj_sb[:, k, :], gates[:, b, 0, :], ALU.mult)\
                            .then_inc(scaled_done, 1)
                        g.tensor_tensor(wbase_s[b][:, k, :], wbase_sb[:, k, :], gates[:, b, 1, :], ALU.mult)\
                            .then_inc(scaled_done, 1)
                    g.tensor_tensor(wup_s[b][:, :], wup_sb, gates[0:NG + 1, b, 1, :], ALU.mult)\
                        .then_inc(scaled_done, 1)
                    g.tensor_tensor(brow[b][:, :], bproj_sb, gates[:, b, 0, :], ALU.mult)\
                        .then_inc(scaled_done, 1)
                pool.wait_ge(scaled_done, 12)

            def rstd(u, stats, step_sem, per, mv, ve, rst, bias, free, done):
                need(pool, done, 2 * u)
                need(pool, free, u)
                pool.wait_ge(stats, 2 * u + 2)
                link, count = steps(pool, step_sem, per * u)
                link(g.tensor_tensor(ve[:, 0, :], mv[:, 4, :], lnc[:, 0, :], ALU.add))
                link(g.tensor_tensor(ve[:, 1, :], ve[:, 0, :], lnc[:, 1, :], ALU.pow))
                link(g.tensor_tensor(ve[:, 2, :], mv[:, 0, :], ve[:, 1, :], ALU.mult))
                assert count[0] == per
                g.tensor_tensor(rst[:, :], ve[:, 1, :], lnc[:, 2, :], ALU.mult).then_inc(done, 1)
                g.tensor_tensor(bias[:, :], ve[:, 2, :], lnc[:, 3, :], ALU.mult).then_inc(done, 1)

            def stage(c_unit, b_unit, a_unit):
                if c_unit:
                    rstd(c_unit[0], statsC, pc_step, PC_STEPS, mvC, veC, rstdC, biasC, xhatC_done, rstdC_done)
                if a_unit is not None:
                    rstd(a_unit, statsA, pa_step, PA_STEPS, mvA, veA, rstdA, biasA, xhatA_done, rstdA_done)
                if b_unit:
                    u, b = b_unit
                    chunk = u - CHUNKS * b
                    pool.wait_ge(kpre_done, b + 1)
                    for n, k in enumerate(QK_P):
                        need(pool, pprod_used, NP * u + n - PSLOTS + 1)
                        g.tensor_tensor(pring[n % PSLOTS][:, :].rearrange("p (h t) -> p h t", h=HALVES),
                                        queriesT[:, :, ds(CW * chunk, CW)],
                                        keysT[b][:, :, ds(PRE * P - COLS[k] + CW * chunk, CW)], ALU.mult)\
                            .then_inc(pprod_done, 1)
                    pool.wait_ge(probs_done, u + 1)
                    pool.wait_ge(a_read, values_there(b))
                    for n, k in enumerate(PV_P):
                        m = len(QK_P) + n
                        pool.wait_ge(pprod_used, NP * u + m - PSLOTS + 1)
                        g.tensor_tensor(
                            pring[m % PSLOTS][:, :].rearrange("p (a d) -> p a d", d=DH),
                            probs[:, k, :].unsqueeze(2).broadcast_to([P, CT * HEADS, DH]),
                            vals[b][:, ds((PRE - BACK[k]) * D + CT * D * chunk, CT * D)]
                            .rearrange("p (a d) -> p a d", d=DH), ALU.mult).then_inc(pprod_done, 1)
                        if n == 1:
                            pool.wait_ge(xb_in, 16 * u + 16)
                            g.tensor_tensor(xb[:, :, :], xb[:, :, :],
                                            brow[b][:, :].unsqueeze(1).broadcast_to([P, CT, D]), ALU.add)\
                                .then_inc(xb_pre, 1)

            setup()
            stage(None, None, 0)
            scale_weights()
            with pool.Fori(1, CHUNKS) as u:
                stage(None, None, u)
            stage(None, (0, 0), CHUNKS)
            with pool.Fori(1, CHUNKS) as u:
                stage((u - 1, 0), (u, 0), u + CHUNKS)
            stage((CHUNKS - 1, 0), (CHUNKS, 1), None)
            with pool.Fori(CHUNKS + 1, UNITS) as u:
                stage((u - 1, 1), (u, 1), None)
            stage((UNITS - 1, 1), None, None)

        @block.scalar
        def _(act):
            s = nc.scalar

            def normalise(u, x_buf, xhat, rst, bias, ready, free, free_value, done):
                act.wait_ge(ready, 2 * u + 2)
                need(act, free, free_value)
                for t in range(CT):
                    ins = s.activation(xhat[:, t, :], x_buf[:, t, :], ACT.Identity,
                                       bias=bias[:, t:t + 1], scale=rst[:, t:t + 1])
                ins.then_inc(done, 1)

            def evac_a(u, b, group, dst, bank_n, func=ACT.Identity, **kw):
                act.wait_ge(a_full, a_base(u, b) + group + 1)
                s.activation(dst, pA[bank_n][:, :], func, **kw).then_inc(a_read, 1)

            def stage(c_unit, b_unit, a_unit):
                if c_unit:
                    cu = c_unit[0]
                    need(act, out_done, 16 * cu)
                    normalise(cu, xb, xhatC, rstdC, biasC, rstdC_done, h2T_full, 2 * cu, xhatC_done)
                if a_unit:
                    au, ab = a_unit
                    achunk = au - CHUNKS * ab
                    normalise(au, xa, xhatA, rstdA, biasA, rstdA_done, a_full,
                              a_base(au - 1, ab) + 2, xhatA_done)
                if c_unit:
                    for k in range(HALVES):
                        act.wait_ge(h2T_full, 2 * cu + k + 1)
                        s.activation(h2T[:, k, :], pB[k][:, :], ACT.Identity, bias=modT[:, 2, k, c_unit[1]:c_unit[1] + 1],
                                     scale=modT[:, 3, k, c_unit[1]:c_unit[1] + 1]).then_inc(h2T_read, 1)
                if a_unit:
                    for k in range(HALVES):
                        evac_a(au, ab, k, hT[:, k, :], k, bias=modT[:, 0, k, ab:ab + 1],
                               scale=modT[:, 1, k, ab:ab + 1])
                if b_unit:
                    bu, bb = b_unit
                    act.wait_ge(vprod_used, NV * bu + len(QK_V))
                    act.wait_ge(pprod_used, NP * bu + len(QK_P))
                    for k in range(HALVES):
                        s.activation(scoresT[:, k, :], pS[k][0:ND * HH, :], ACT.Copy).then_inc(sT_read, 1)
                if c_unit:
                    act.wait_ge(lsub_done, cu + 1)
                    s.activation(lexp[:, :, :], lsub[:, :, :], ACT.Exp).then_inc(lexp_done, 1)

                def keys(k):
                    evac_a(au, ab, 2 + k, keysT[ab][:, k, ds(PRE * P + CW * achunk, CW)], k,
                           bias=bqkv_sb[:, 2 + k:3 + k])

                def queries(k):
                    if ab and not k:
                        act.wait_ge(vprod_done, NV * (au - CHUNKS) + len(QK_V))
                        act.wait_ge(pprod_done, NP * (au - CHUNKS) + len(QK_P))
                    evac_a(au, ab, 4 + k, queriesT[:, k, ds(CW * achunk, CW)], k, bias=bqkv_sb[:, k:k + 1])

                if a_unit:
                    keys(0)
                if b_unit:
                    act.wait_ge(ssub_done, bu + 1)
                    s.activation(probs[:, :, :], probs[:, :, :], ACT.Exp, scale=SCALE).then_inc(exp_done, 1)
                if a_unit:
                    keys(1)
                if c_unit:
                    act.wait_ge(loraT_full, cu + 1)
                    s.activation(loraT[:, :], pB[1][0:NG + 1, :], ACT.Copy).then_inc(loraT_read, 1)
                if a_unit:
                    queries(0)
                    queries(1)
                if b_unit:
                    act.wait_ge(vprod_used, NV * bu + NV)
                    act.wait_ge(pprod_used, NP * bu + NP)
                    for k in range(HALVES):
                        s.activation(attnT[:, k, :], pO[k][:, :], ACT.Identity,
                                     bias=bqkv_sb[:, 4 + k:5 + k]).then_inc(attnT_read, 1)
                if a_unit:
                    for n in range(2):
                        evac_a(au, ab, 6 + n, vals[ab][:, ds((PRE + 2 * n) * D + CT * D * achunk, 2 * D)], n,
                               ACT.Copy)

            def prefix(b):
                act.wait_ge(a_read, a_base(CHUNKS * (b + 1), b))
                s.activation(keysT[b][:, :, 0:PRE * P], keysT[b][:, :, (TILES * P - 1):(TILES + PRE) * P - 1],
                             ACT.Copy).then_inc(kpre_done, 1)
                for n in range(4):
                    act.wait_ge(a_full, a_base(CHUNKS * (b + 1), b) + n + 1)
                    s.activation(vals[b][:, 2 * n * D:2 * (n + 1) * D], pA[n % 2][:, :], ACT.Copy)\
                        .then_inc(a_read, 1)

            act.wait_ge(ld_mod, 32)
            s.activation(silu[:, 0, :, :], cT_sb[:, :, :], ACT.Exp, scale=-1.0).then_inc(expc_done, 1)
            act.wait_ge(modT_done, 2)
            act.wait_ge(ld_qkv, 48)
            stage(None, None, (0, 0))
            with act.Fori(1, CHUNKS) as u:
                stage(None, None, (u, 0))
            prefix(0)
            act.wait_ge(scaled_done, 12)
            stage(None, (0, 0), (CHUNKS, 1))
            with act.Fori(1, CHUNKS) as u:
                stage((u - 1, 0), (u, 0), (u + CHUNKS, 1))
            prefix(1)
            stage((CHUNKS - 1, 0), (CHUNKS, 1), None)
            with act.Fori(CHUNKS + 1, UNITS) as u:
                stage((u - 1, 1), (u, 1), None)
            stage((UNITS - 1, 1), None, None)

        @block.vector
        def _(dve):
            v = nc.vector

            def setup():
                link, _ = steps(dve, setup_v, 0)
                dve.wait_ge(expc_done, 1)
                link(v.tensor_scalar(silu[:, 1, :, :], silu[:, 0, :, :], 1.0, None, ALU.add))
                link(v.reciprocal(silu[:, 2, :, :], silu[:, 1, :, :]))
                link(v.tensor_tensor(silu[:, 0, :, :], cT_sb[:, :, :], silu[:, 2, :, :], ALU.mult))
                v.tensor_copy(silub, silu[:, 0, :, :].unsqueeze(3).broadcast_to([P, HALVES, BATCH, P]))\
                    .then_inc(silu_done, 1)
                dve.wait_ge(mod_full, 1)
                shift_scale = pO[0][:, 0:16].rearrange("p (v s k b) -> p v s k b", v=2, s=2, k=HALVES)
                m = modT[:, :, :, :].rearrange("p (v s) k b -> p v s k b", s=2)
                v.tensor_copy(m[:, :, 0, :, :], shift_scale[:, :, 0, :, :]).then_inc(modT_done, 1)
                v.tensor_scalar(m[:, :, 1, :, :], shift_scale[:, :, 1, :, :], 1.0, None, ALU.add)\
                    .then_inc(modT_done, 1)

            def gate_rows():
                link, _ = steps(dve, setup_v, 3)
                for b in range(BATCH):
                    src = pS[b][:, :].rearrange("p (v n) -> p v n", v=2)
                    link(v.tensor_scalar(gsign[:, b, :, :], src, 0.0, 2.0, ALU.is_ge, ALU.mult))
                    link(v.scalar_tensor_tensor(gates[:, b, :, :], gsign[:, b, :, :], -1.0, src, ALU.add,
                                                ALU.mult))
                    link(v.tensor_scalar(gates[:, b, :, :], gates[:, b, :, :], 0.25, None, ALU.max))
                v.scalar_tensor_tensor(gates, gsign, -1.0, gates, ALU.add, ALU.mult).then_inc(gates_done, 1)

            def stats(u, x_buf, bn, mv, step_sem, base, free, done):
                need(dve, free, 2 * u)
                for t in range(CT):
                    v.bn_stats(bn[:, t, :], x_buf[:, t, :]).then_inc(step_sem, 1)
                dve.wait_ge(step_sem, base + CT)
                v.tensor_tensor(mv[:, 0, :], bn[:, :, 1], bn[:, :, 4], ALU.add).then_inc(done, 1)
                v.tensor_tensor(mv[:, 1, :], bn[:, :, 2], bn[:, :, 5], ALU.add).then_inc(step_sem, 1)
                v.tensor_tensor(mv[:, 2, :], bn[:, :, 1], bn[:, :, 4], ALU.subtract).then_inc(step_sem, 1)
                dve.wait_ge(step_sem, base + CT + 2)
                v.scalar_tensor_tensor(mv[:, 3, :], mv[:, 2, :], D / 4, mv[:, 2, :], ALU.mult, ALU.mult)\
                    .then_inc(step_sem, 1)
                dve.wait_ge(step_sem, base + CT + 3)
                v.tensor_tensor(mv[:, 4, :], mv[:, 1, :], mv[:, 3, :], ALU.add).then_inc(done, 1)

            def stage(c_unit, b_unit, a_unit):
                if c_unit:
                    cu = c_unit[0]
                    dve.wait_ge(xb_pre, cu + 1)
                    for n in range(2):
                        dve.wait_ge(y_full, 2 * cu + n + 1)
                        part = xb[:, 2 * n:2 * n + 2, :]
                        v.tensor_tensor(part, pB[n][:, :].rearrange("p (t c) -> p t c", c=D), part, ALU.add)\
                            .then_inc(y_read, 1)
                    dve.wait_ge(y_read, 2 * cu + 2)
                    stats(cu, xb, bnC, mvC, vc_step, VC_STEPS * cu, rstdC_done, statsC)
                if a_unit is not None:
                    dve.wait_ge(xa_in, 16 * a_unit + 16)
                    stats(a_unit, xa, bnA, mvA, va_step, VA_STEPS * a_unit, rstdA_done, statsA)
                if b_unit:
                    u, b = b_unit
                    chunk = u - CHUNKS * b
                    dve.wait_ge(kpre_done, b + 1)
                    for n, k in enumerate(QK_V):
                        need(dve, vprod_used, NV * u + n - VSLOTS + 1)
                        v.tensor_tensor(vring[n % VSLOTS][:, :].rearrange("p (h t) -> p h t", h=HALVES),
                                        queriesT[:, :, ds(CW * chunk, CW)],
                                        keysT[b][:, :, ds(PRE * P - COLS[k] + CW * chunk, CW)], ALU.mult)\
                            .then_inc(vprod_done, 1)
                if c_unit:
                    router(cu)
                if b_unit:
                    softmax_front(u)
                if c_unit:
                    final(cu)
                if b_unit:
                    softmax_back(u)
                    dve.wait_ge(a_read, values_there(b))
                    for n, k in enumerate(PV_V):
                        m = len(QK_V) + n
                        dve.wait_ge(vprod_used, NV * u + m - VSLOTS + 1)
                        if k == 1:
                            dve.wait_ge(pshift_full, u + 1)
                        pr = probs[:, k, :] if k == 0 else pS[0][:, (k - 1) * CT * HEADS:k * CT * HEADS]
                        v.tensor_tensor(
                            vring[m % VSLOTS][:, :].rearrange("p (a d) -> p a d", d=DH),
                            pr.unsqueeze(2).broadcast_to([P, CT * HEADS, DH]),
                            vals[b][:, ds((PRE - BACK[k]) * D + CT * D * chunk, CT * D)]
                            .rearrange("p (a d) -> p a d", d=DH), ALU.mult).then_inc(vprod_done, 1)

            def softmax_front(u):
                dve.wait_ge(pprod_done, NP * u + len(QK_P))
                need(dve, pshift_full, u)
                G = 2 * HALVES
                link, count = steps(dve, vb_step, VB_STEPS * u)
                for n in range(2):
                    dve.wait_ge(stok_full, 2 * u + n + 1)
                    sc = pO[n][:, 0:G * ND * HH].rearrange("p (g o h) -> p g o h", g=G, o=ND)
                    mx = smax[:, n * 32:n * 32 + 32].rearrange("p (g h) -> p g h", h=HH)
                    link(v.tensor_reduce(mx, sc.rearrange("p g o h -> p g h o"), AX.X, ALU.max))
                    ins = v.tensor_tensor(
                        probs[:, :, n * 32:n * 32 + 32].rearrange("p o (g h) -> p g o h", h=HH), sc,
                        mx.unsqueeze(2).broadcast_to([P, G, ND, HH]), ALU.subtract)
                ins.then_inc(ssub_done, 1)
                assert count[0] == 2

            def softmax_back(u):
                link, count = steps(dve, vb_step, VB_STEPS * u + 2)
                dve.wait_ge(exp_done, u + 1)
                link(v.tensor_reduce(ssum[:, :], probs[:, :, :].rearrange("p o g -> p g o"), AX.X, ALU.add))
                link(v.reciprocal(srec[:, :], ssum[:, :]))
                v.tensor_tensor(probs[:, :, :], probs[:, :, :],
                                srec[:, :].unsqueeze(1).broadcast_to([P, ND, CT * HEADS]), ALU.mult)\
                    .then_inc(probs_done, 1)
                dve.wait_ge(probs_done, u + 1)
                assert count[0] == 2

            def router(u):
                link, count = steps(dve, vc_step, VC_STEPS * u + CT + 3)
                dve.wait_ge(down_full, u + 1)
                down = pB[0][:, 0:CT * NA].rearrange("p (t n) -> p t n", n=NA)
                link(v.tensor_tensor(lg[:, :, :], down[:, :, NG:NA],
                                     rb_sb[:, :].unsqueeze(1).broadcast_to([P, CT, E]), ALU.add))
                link(v.tensor_reduce(lmax[:, :], lg[:, :, :], AX.X, ALU.max))
                v.tensor_tensor(lsub[:, :, :], lg[:, :, :], lmax[:, :].unsqueeze(2).broadcast_to([P, CT, E]),
                                ALU.subtract).then_inc(lsub_done, 1)
                other = lg[:, :, :].unsqueeze(2).broadcast_to([P, CT, E, E])
                own = lg[:, :, :].unsqueeze(3).broadcast_to([P, CT, E, E])
                link(v.tensor_tensor(level[:, :, :, :], other, own, ALU.is_ge))
                link(v.tensor_tensor(above[:, :, :, :], other, own, ALU.is_gt))
                link(v.tensor_tensor(level[:, :, :, :], level[:, :, :, :],
                                     lower_sb[:, :, :].unsqueeze(1).broadcast_to([P, CT, E, E]), ALU.mult))
                link(v.tensor_tensor(above[:, :, :, :], above[:, :, :, :], level[:, :, :, :], ALU.max))
                link(v.tensor_reduce(rank[:, :, :], above[:, :, :, :], AX.X, ALU.add))
                dve.wait_ge(lexp_done, u + 1)
                link(v.scalar_tensor_tensor(picked[:, :, :], rank[:, :, :], TOPK - 0.5, lexp[:, :, :],
                                            ALU.is_lt, ALU.mult))
                link(v.tensor_reduce(zall[:, :], lexp[:, :, :], AX.X, ALU.add))
                link(v.tensor_reduce(zpick[:, :], picked[:, :, :], AX.X, ALU.add))
                link(v.scalar_tensor_tensor(zall[:, :], zall[:, :], 1e-6, zpick[:, :], ALU.mult, ALU.add))
                link(v.reciprocal(zrec[:, :], zall[:, :]))
                link(v.tensor_tensor(wsel[:, :, :], picked[:, :, :],
                                     zrec[:, :].unsqueeze(2).broadcast_to([P, CT, E]), ALU.mult))
                need(dve, loraT_full, u)
                v.tensor_tensor(lora[:, :, 0:NR].rearrange("p t (e r) -> p t e r", r=R),
                                down[:, :, 0:NR].rearrange("p t (e r) -> p t e r", r=R),
                                wsel[:, :, :].unsqueeze(3).broadcast_to([P, CT, E, R]), ALU.mult)\
                    .then_inc(lora_done, 1)
                v.tensor_copy(lora[:, :, NR:NG], down[:, :, NR:NG]).then_inc(lora_done, 1)
                assert count[0] == VC_STEPS - CT - 3

            def final(u):
                for n in range(2):
                    dve.wait_ge(y2_full, 2 * u + n + 1)
                    v.tensor_tensor(x2[:, 2 * n:2 * n + 2, :], pB[n][:, :].rearrange("p (t c) -> p t c", c=D),
                                    xb[:, 2 * n:2 * n + 2, :], ALU.add).then_inc(y2_read, 1)

            stage(None, None, 0)
            setup()
            gate_rows()
            with dve.Fori(1, CHUNKS) as u:
                stage(None, None, u)
            stage(None, (0, 0), CHUNKS)
            with dve.Fori(1, CHUNKS) as u:
                stage((u - 1, 0), (u, 0), u + CHUNKS)
            stage((CHUNKS - 1, 0), (CHUNKS, 1), None)
            with dve.Fori(CHUNKS + 1, UNITS) as u:
                stage((u - 1, 1), (u, 1), None)
            stage((UNITS - 1, 1), None, None)

        @block.tensor
        def _(pe):
            t_ = nc.tensor
            ident = perm_sb[:, 0, :]

            def a_group(u, b, group):
                need(pe, a_read, a_base(u, b) + group - 1)
                return pA[group % 2]

            def stage(c_unit, b_unit, a_unit):
                if b_unit:
                    u, b = b_unit
                    chunk = u - CHUNKS * b
                if a_unit:
                    au, ab = a_unit
                if c_unit:
                    cu, cb = c_unit

                def hT_transposes():
                    pe.wait_ge(xhatA_done, au + 1)
                    for k in range(HALVES):
                        dst = a_group(au, ab, k)
                        for t in range(CT):
                            ins = t_.transpose(dst[:, t * P:(t + 1) * P], xhatA[:, t, k * P:(k + 1) * P], ident)
                        ins.then_inc(a_full, 1)

                def project_T(group, col):
                    dst = a_group(au, ab, group)
                    for k in range(HALVES):
                        ins = t_.matmul(dst[:, :], wqkv_sb[:, k, col:col + P], hT[:, k, :], start=(k == 0),
                                        stop=(k == HALVES - 1))
                    ins.then_inc(a_full, 1)

                def keys(k):
                    if k == 0:
                        pe.wait_ge(a_read, a_base(au, ab) + 2)
                    project_T(2 + k, D + k * P)

                def queries(k):
                    project_T(4 + k, k * P)

                def values():
                    for n in range(2):
                        dst = a_group(au, ab, 6 + n)
                        for t in range(2):
                            for k in range(HALVES):
                                col = (2 * n + t) * P
                                ins = t_.matmul(dst[:, t * D:(t + 1) * D], hT[:, k, col:col + P],
                                                wqkv_sb[:, k, 2 * D:3 * D], start=(k == 0),
                                                stop=(k == HALVES - 1))
                        ins.then_inc(a_full, 1)

                def scores(rounds):
                    for r in rounds:
                        if r == 0:
                            need(pe, sT_read, 2 * u)
                            need(pe, vprod_done, NV * u)
                            for h in range(HALVES):
                                t_.matmul(pS[h][0:ND * HH, :], maskrow_sb[:, :], mask_sb[:, ds(CW * chunk, CW)],
                                          start=True, stop=False, skip_group_check=True)
                        vn, pn = (sum(e == w for rr in QK_ROUNDS[:r + 1] for e, _ in rr) for w in "vp")
                        pe.wait_ge(vprod_done, NV * u + vn)
                        pe.wait_ge(pprod_done, NP * u + pn)
                        for h in range(HALVES):
                            for e, k in QK_ROUNDS[r]:
                                src = (vring[QK_V.index(k) % VSLOTS] if e == "v" else
                                       pring[QK_P.index(k) % PSLOTS])
                                q = k // 4
                                ins = t_.matmul(pS[h][32 * q:32 * q + 32, :], sel_sb[:, k % 4, :],
                                                src[:, h * CW:(h + 1) * CW], start=False,
                                                stop=(r == 3), skip_group_check=True)
                                if h == HALVES - 1:
                                    ins.then_inc(vprod_used if e == "v" else pprod_used, 1)

                def score_transposes():
                    pe.wait_ge(sT_read, 2 * u + 2)
                    need(pe, attnT_read, 2 * u)
                    for t in range(CT):
                        for h in range(HALVES):
                            at = ((t % 2) * HALVES + h) * ND * HH
                            ins = t_.transpose(pO[t // 2][:, at:at + ND * HH],
                                               scoresT[:, h, t * P:(t + 1) * P],
                                               perm_sb[0:ND * HH, 0, 0:ND * HH])
                        if t % 2:
                            ins.then_inc(stok_full, 1)

                def shift_probs():
                    pe.wait_ge(probs_done, u + 1)
                    for k in range(1, 1 + NSH):
                        ins = t_.matmul(pS[0][:, (k - 1) * CT * HEADS:k * CT * HEADS], permT_sb[:, k - 1, :],
                                        probs[:, k, :], start=True, stop=True)
                    ins.then_inc(pshift_full, 1)

                def attend():
                    nv, np_ = len(QK_V), len(QK_P)
                    for i, (e, k) in enumerate(PV_ORDER):
                        if e == "v":
                            src, nv = vring[nv % VSLOTS], nv + 1
                            pe.wait_ge(vprod_done, NV * u + nv)
                        else:
                            src, np_ = pring[np_ % PSLOTS], np_ + 1
                            pe.wait_ge(pprod_done, NP * u + np_)
                        place = perm_sb[:, PERMS.index(SHIFT[k]), :]
                        for t in range(CT):
                            for h in range(HALVES):
                                at = t * D + h * P
                                ins = t_.matmul(pO[h][:, t * P:(t + 1) * P], src[:, at:at + P], place,
                                                start=(i == 0 and t == 0), stop=(i == ND - 1),
                                                is_transpose=True, skip_group_check=True)
                        ins.then_inc(vprod_used if e == "v" else pprod_used, 1)

                def project():
                    pe.wait_ge(attnT_read, 2 * u + 2)
                    pe.wait_ge(scaled_done, 12)
                    for n in range(2):
                        need(pe, y2_read, 2 * u - 1 + n)
                        for t in range(2):
                            for k in range(HALVES):
                                col = (2 * n + t) * P
                                ins = t_.matmul(pB[n][:, t * D:(t + 1) * D], attnT[:, k, col:col + P],
                                                wproj_s[b][:, k, :], start=(k == 0), stop=(k == HALVES - 1))
                        ins.then_inc(y_full, 1)

                def h2T_transposes():
                    pe.wait_ge(xhatC_done, cu + 1)
                    for k in range(HALVES):
                        pe.wait_ge(y_read, 2 * cu + 1 + k)
                        for t in range(CT):
                            ins = t_.transpose(pB[k][:, t * P:(t + 1) * P], xhatC[:, t, k * P:(k + 1) * P],
                                               ident)
                        ins.then_inc(h2T_full, 1)

                def down():
                    pe.wait_ge(h2T_read, 2 * cu + 2)
                    for t in range(CT):
                        for k in range(HALVES):
                            ins = t_.matmul(pB[0][:, t * NA:(t + 1) * NA], h2T[:, k, t * P:(t + 1) * P],
                                            wdown_sb[:, k, :], start=(k == 0), stop=(k == HALVES - 1))
                    ins.then_inc(down_full, 1)

                def lora_transposes():
                    pe.wait_ge(lora_done, 2 * cu + 2)
                    for t in range(CT):
                        ins = t_.transpose(pB[1][0:NG + 1, t * P:(t + 1) * P], lora[:, t, :], ident)
                    ins.then_inc(loraT_full, 1)

                def up():
                    for n in range(2):
                        if n == 0:
                            pe.wait_ge(lora_done, 2 * cu + 2)
                        pe.wait_ge(loraT_read, cu + 1)
                        for t in range(2):
                            col = (2 * n + t) * P
                            dst = pB[n][:, t * D:(t + 1) * D]
                            for k in range(HALVES):
                                t_.matmul(dst, h2T[:, k, col:col + P], wbase_s[cb][:, k, :], start=(k == 0),
                                          stop=False)
                            ins = t_.matmul(dst, loraT[:, col:col + P], wup_s[cb][:, :], start=False, stop=True)
                        ins.then_inc(y2_full, 1)

                if b_unit:
                    scores([0, 1])
                if c_unit:
                    h2T_transposes()
                if a_unit:
                    hT_transposes()
                if c_unit:
                    down()
                if b_unit:
                    scores([2, 3])
                    score_transposes()
                if a_unit:
                    keys(0)
                    keys(1)
                if c_unit:
                    lora_transposes()
                    up()
                if a_unit:
                    queries(0)
                if b_unit:
                    shift_probs()
                if a_unit:
                    queries(1)
                if b_unit:
                    attend()
                if a_unit:
                    values()
                if b_unit:
                    project()

            def prefix(b):
                pe.wait_ge(a_read, a_base(CHUNKS * (b + 1), b))
                for n in range(4):
                    need(pe, a_read, a_base(CHUNKS * (b + 1), b) + n - 1)
                    at = (PRE + 8 + 2 * n) * D
                    t_.matmul(pA[n % 2][:, :], perm_sb[:, 1, :], vals[b][:, at:at + 2 * D], start=True,
                              stop=True).then_inc(a_full, 1)

            pe.wait_ge(silu_done, 1)
            pe.wait_ge(ld_mod, 32)
            for b in range(BATCH):
                for n, vec in enumerate((2, 5)):
                    for k in range(HALVES):
                        t_.matmul(pS[b][:, n * D:(n + 1) * D], silub[:, k, b, :],
                                  wmod_sb[:, k, vec * D:(vec + 1) * D], start=(k == 0), stop=(k == 1))
            for n, vec in enumerate((0, 1, 3, 4)):
                for h in range(HALVES):
                    at = (n * HALVES + h) * BATCH
                    for k in range(HALVES):
                        col = vec * D + h * P
                        ins = t_.matmul(pO[0][:, at:at + BATCH], wmod_sb[:, k, col:col + P],
                                        silu[:, 0, k, :], start=(k == 0), stop=(k == 1))
            ins.then_inc(mod_full, 1)
            pe.wait_ge(ld_qkv, 48)
            stage(None, None, (0, 0))
            with pe.Fori(1, CHUNKS) as u:
                stage(None, None, (u, 0))
            prefix(0)
            pe.wait_ge(ld_const, 16 * 7)
            pe.wait_ge(gates_done, 1)
            pe.wait_ge(const_done, 5)
            stage(None, (0, 0), (CHUNKS, 1))
            with pe.Fori(1, CHUNKS) as u:
                stage((u - 1, 0), (u, 0), (u + CHUNKS, 1))
            prefix(1)
            stage((CHUNKS - 1, 0), (CHUNKS, 1), None)
            with pe.Fori(CHUNKS + 1, UNITS) as u:
                stage((u - 1, 1), (u, 1), None)
            stage((UNITS - 1, 1), None, None)


def kernel(**inputs):
    import numpy as np
    import concourse.bacc as bacc
    from ml_dtypes import bfloat16 as bf16
    from concourse.bass_utils import run_bass_kernel_spmd

    f = {k.replace("L0_attn_", "").replace("L0_ffn_", "").replace("L0_", ""): np.ascontiguousarray(v)
         for k, v in inputs.items()}
    perm = np.zeros((P, len(PERMS), P), np.float32)
    for n, m in enumerate(PERMS):
        perm[np.arange(P), n, (np.arange(P) + m) % P] = 1.0
    permT = np.zeros((P, NSH, P), np.float32)
    for n in range(NSH):
        permT[(np.arange(P) + SHIFT[1 + n]) % P, n, np.arange(P)] = 1.0
    sel = np.zeros((P, 4, 32), np.float32)
    for n in range(4):
        sel[np.arange(P), n, n * HH + np.arange(P) // DH] = 1.0
    token = (np.arange(TILES)[:, None] + TILES * np.arange(P)[None, :]).reshape(-1)
    mask = np.where(token[None, :] < np.array(DIST)[:, None], MASKED, 0.0).astype(bf16)
    maskrow = (np.arange(ND)[:, None] == np.arange(ND * HH)[None, :] // HH).astype(bf16)
    lower = np.broadcast_to((np.arange(E)[None, :] < np.arange(E)[:, None]).astype(np.float32), (P, E, E))
    arrays = {
        "x": f["x"],
        "cT": f["c"].T.reshape(HALVES, P, BATCH).transpose(1, 0, 2),
        "wmod": f["wmod"],
        "wqkv": f["W_qkv"],
        "bqkv": f["b_qkv"].reshape(3 * HALVES, P).T,
        "wproj": f["W_proj"],
        "bproj": f["b_proj"],
        "wbase": f["base_W"].T,
        "wdown": np.concatenate([f["routed_A"].reshape(NR, D), f["shared_A"], f["router_W"]]).T,
        "wup": np.concatenate([f["routed_B"].transpose(0, 2, 1).reshape(NR, D), f["shared_B"].T,
                               f["base_b"][None, :]]),
        "rb": f["router_b"],
        "perm": perm, "permT": permT, "sel": sel, "mask": mask, "maskrow": maskrow, "lower": lower,
    }
    arrays = {f"in_{k}": np.ascontiguousarray(a) for k, a in arrays.items()}
    nc = bacc.Bacc("TRN2", target_bir_lowering=False, num_devices=1)
    args = [nc.dram_tensor(k, a.shape, mybir.dt.from_np(a.dtype), kind="ExternalInput").ap()
            for k, a in arrays.items()]
    args.append(nc.dram_tensor("out", f["x"].shape, F32, kind="ExternalOutput").ap())
    build(nc, *args)
    r = run_bass_kernel_spmd(nc, [arrays], core_ids=[0])
    return r.results[0]["out"]
```

```python
from contextlib import ExitStack

import concourse.bass as bass
from concourse import mybir

F32 = mybir.dt.float32
BF16 = mybir.dt.bfloat16
ALU = mybir.AluOpType
ACT = mybir.ActivationFunctionType
AX = mybir.AxisListType

P = 128
BATCH, SEQ, D = 2, 2048, 256
HEADS, DH = 16, 16
HALVES = D // P
HH = HEADS // HALVES
TILES = SEQ // P
CT = 4
CHUNKS = TILES // CT
CW = CT * P
UNITS = BATCH * CHUNKS
PRE = 8
E, R, TOPK = 6, 16, 2
NR = E * R
NG = NR + R
NA = NG + E
SCALE = DH ** -0.5
EPS = 1e-5
MASKED = -1e30

DIST = [0, 16, 32, 64, 128, 256, 512, 1024, 1, 2, 4, 8]
ND = len(DIST)
SHIFT = [d // 16 for d in DIST]
BACK = [d if d < 16 else 0 for d in DIST]
COLS = [d * P if d < 16 else d // 16 for d in DIST]
PERMS = [0, 1, 2, 4, 8, 16, 32, 64]
NSH = 7

QK_ROUNDS = [[("v", r), ("v", 4 + r), ("p", 8 + r)] for r in range(4)]
PV_ORDER = [("v", 0), ("p", 8), ("v", 1), ("v", 2), ("p", 9), ("v", 3), ("v", 4), ("p", 10), ("v", 5),
            ("v", 6), ("p", 11), ("v", 7)]
QK_V = [k for r in QK_ROUNDS for e, k in r if e == "v"]
QK_P = [k for r in QK_ROUNDS for e, k in r if e == "p"]
PV_V = [k for e, k in PV_ORDER if e == "v"]
PV_P = [k for e, k in PV_ORDER if e == "p"]
VSLOTS, PSLOTS = 4, 2
VBURST, PBURST = 2 * VSLOTS, 2 * PSLOTS
assert len(QK_V) == len(PV_V) == VBURST and len(QK_P) == len(PV_P) == PBURST

VA_STEPS, VB_STEPS, VC_STEPS = 7, 4, 20
PA_STEPS, PC_STEPS = 3, 3


def ds(start, size):
    return bass.ds(start, size)


def build(nc, x, cT, wmod, wqkv, bqkv, wproj, bproj, wbase, wdown, wup, rb, perm, permT, sel, mask, maskrow,
          lower, out):
    x_v = x.rearrange("b (p j) c -> b p j c", j=TILES)
    out_v = out.rearrange("b (p j) c -> b p j c", j=TILES)

    with ExitStack() as ctx:
        def sb(name, shape, dt=F32):
            return ctx.enter_context(nc.sbuf_tensor(name, shape, dt))

        def bank(name):
            return ctx.enter_context(nc.psum_tensor(name, [P, 512], F32))

        def sem(name):
            return ctx.enter_context(nc.semaphore(name))

        KW = (PRE + TILES) * P
        keysT = [sb(f"keysT{b}", [P, HALVES, KW]) for b in range(BATCH)]
        vals = [sb(f"vals{b}", [P, (PRE + TILES) * D]) for b in range(BATCH)]
        queriesT = sb("queriesT", [P, HALVES, SEQ])
        vring = [sb(f"vprod{s}", [P, 2 * CW]) for s in range(VSLOTS)]
        pring = [sb(f"pprod{s}", [P, 2 * CW]) for s in range(PSLOTS)]
        xa = sb("xa", [P, CT, D])
        xb = sb("xb", [P, CT, D])
        xhatA = sb("xhatA", [P, CT, D])
        hT = sb("hT", [P, HALVES, CW])
        x2 = sb("x2", [P, CT, D])
        xhatC = x2
        h2T = sb("h2T", [P, HALVES, CW])
        probs = sb("probs", [P, ND, CT * HEADS])
        shifted = sb("shifted", [P, NSH, CT * HEADS])
        attnT = sb("attnT", [P, HALVES, CW])
        scoresT = attnT[0:ND * HH, :, :]
        smax = sb("smax", [P, CT * HEADS])
        ssum = sb("ssum", [P, CT * HEADS])
        srec = sb("srec", [P, CT * HEADS])
        bnA = sb("bnA", [P, CT, 6])
        mvA = sb("mvA", [P, 5, CT])
        bnC = sb("bnC", [P, CT, 6])
        mvC = sb("mvC", [P, 5, CT])
        veA = sb("veA", [P, 3, CT])
        veC = sb("veC", [P, 3, CT])
        rstdA = sb("rstdA", [P, CT])
        rstdC = sb("rstdC", [P, CT])
        biasA = sb("biasA", [P, CT])
        biasC = sb("biasC", [P, CT])
        lnc = sb("lnc", [P, 4, CT])
        lg = sb("lg", [P, CT, E])
        lmax = sb("lmax", [P, CT])
        lsub = sb("lsub", [P, CT, E])
        lexp = sb("lexp", [P, CT, E])
        above = sb("above", [P, CT, E, E])
        level = sb("level", [P, CT, E, E])
        rank = sb("rank", [P, CT, E])
        picked = sb("picked", [P, CT, E])
        zall = sb("zall", [P, CT])
        zpick = sb("zpick", [P, CT])
        zrec = sb("zrec", [P, CT])
        wsel = sb("wsel", [P, CT, E])
        lora = sb("lora", [P, CT, NG + 1])
        loraT = sb("loraT", [NG + 1, CW])
        wqkv_sb = sb("wqkv_sb", [P, HALVES, 3 * D])
        bqkv_sb = sb("bqkv_sb", [P, 3 * HALVES])
        wdown_sb = sb("wdown_sb", [P, HALVES, NA])
        wproj_s = [sb(f"wproj_s{b}", [P, HALVES, D]) for b in range(BATCH)]
        wbase_s = [sb(f"wbase_s{b}", [P, HALVES, D]) for b in range(BATCH)]
        wup_s = [sb(f"wup_s{b}", [NG + 1, D]) for b in range(BATCH)]
        brow = [sb(f"brow{b}", [P, D]) for b in range(BATCH)]
        rb_sb = sb("rb_sb", [P, E])
        lower_sb = sb("lower_sb", [P, E, E])
        perm_sb = sb("perm_sb", [P, len(PERMS), P])
        permT_sb = sb("permT_sb", [P, NSH, P])
        sel_sb = sb("sel_sb", [P, 4, 32])
        mask_sb = sb("mask_sb", [ND, SEQ], BF16)
        maskrow_sb = sb("maskrow_sb", [ND, ND * HH], BF16)
        cT_sb = sb("cT_sb", [P, HALVES, BATCH])
        silu = sb("silu", [P, 3, HALVES, BATCH])
        modT = sb("modT", [P, 4, HALVES, BATCH])
        room = vals[1]
        wmod_sb = room[:, 0:2 * 6 * D].rearrange("p (k n) -> p k n", k=HALVES)
        at = 2 * 6 * D
        wproj_sb = room[:, at:at + 2 * D].rearrange("p (k n) -> p k n", k=HALVES)
        at += 2 * D
        wbase_sb = room[:, at:at + 2 * D].rearrange("p (k n) -> p k n", k=HALVES)
        at += 2 * D
        wup_sb = room[0:NG + 1, at:at + D]
        at += D
        bproj_sb = room[:, at:at + D]
        at += D
        gates = room[:, at:at + 4 * D].rearrange("p (b v n) -> p b v n", b=BATCH, v=2)
        gsign = vring[0][:, :].rearrange("p (b v n) -> p b v n", b=BATCH, v=2)
        silub = vring[1][:, 0:4 * P].rearrange("p (k b n) -> p k b n", k=HALVES, b=BATCH)

        PROD = 2 * CW
        first_keys = keysT[0][:, :, :].rearrange("p k n -> p (k n)")
        kroom = [first_keys[:, s * PROD:(s + 1) * PROD] for s in range(VSLOTS + PSLOTS)]
        vroom = [vals[0][:, s * PROD:(s + 1) * PROD] for s in range(VSLOTS + PSLOTS)]
        xr = hT[:, :, :].rearrange("p k (t c) -> p (k t) c", c=D)

        pS = [bank("pS0"), bank("pS1")]
        pO = [bank("pO0"), bank("pO1")]
        pB = [bank("pB0"), bank("pB1")]
        pA = [bank("pA0"), bank("pA1")]

        ld_mod, ld_rest, ld_qkv, ld_const, ld_scaled = (sem(n) for n in
                                                         ("ld_mod", "ld_rest", "ld_qkv", "ld_const", "ld_scaled"))
        xa_in, xb_in, out_done = sem("xa_in"), sem("xb_in"), sem("out_done")
        expc_done, silu_done, mod_full, modT_done, gates_done, scaled_done = (
            sem(n) for n in ("expc_done", "silu_done", "mod_full", "modT_done", "gates_done", "scaled_done"))
        const_done, setup_v = sem("const_done"), sem("setup_v")
        statsA, rstdA_done, xhatA_done = sem("statsA"), sem("rstdA_done"), sem("xhatA_done")
        statsC, rstdC_done, xhatC_done = sem("statsC"), sem("rstdC_done"), sem("xhatC_done")
        a_full, a_read, kpre_done = sem("a_full"), sem("a_read"), sem("kpre_done")
        qkv_done, qkp_done, pvv_done, pvp_done = (sem(n) for n in ("qkv_done", "qkp_done", "pvv_done", "pvp_done"))
        qkv_used, qkp_used, pvv_used, pvp_used = (sem(n) for n in ("qkv_used", "qkp_used", "pvv_used", "pvp_used"))
        sT_read = sem("sT_read")
        stok_full, ssub_done, exp_done, probs_done = (sem(n) for n in
                                                      ("stok_full", "ssub_done", "exp_done", "probs_done"))
        pshift_full, shifted_done, attnT_read = sem("pshift_full"), sem("shifted_done"), sem("attnT_read")
        xb_pre, y_full, y_read = sem("xb_pre"), sem("y_full"), sem("y_read")
        h2T_full, h2T_read = sem("h2T_full"), sem("h2T_read")
        down_full, lsub_done, lexp_done, lora_done = (sem(n) for n in
                                                      ("down_full", "lsub_done", "lexp_done", "lora_done"))
        loraT_full, loraT_read, y2_full, y2_read = (sem(n) for n in
                                                    ("loraT_full", "loraT_read", "y2_full", "y2_read"))
        va_step, vb_step, vc_step, pa_step, pc_step = (sem(n) for n in
                                                       ("va_step", "vb_step", "vc_step", "pa_step", "pc_step"))

        def need(eng, s, value):
            if not isinstance(value, int) or value > 0:
                eng.wait_ge(s, value)

        def steps(eng, s, base):
            count = [0]

            def link(ins):
                count[0] += 1
                ins.then_inc(s, 1)
                eng.wait_ge(s, base + count[0])
            return link, count

        def schedule(eng, a_unit, setup, iteration, c_unit):
            a_unit(0, 0)
            setup()
            with eng.Fori(1, CHUNKS) as u:
                a_unit(u, 0)
            N = CHUNKS
            iteration(None, 0, None, 0, 0, 0, 1, 0, N)
            iteration(0, 0, None, 0, 1, 0, 2, 0, N + 1)
            iteration(1, 0, 0, 0, 2, 0, 3, 0, N + 2)
            iteration(2, 0, 1, 0, 3, 0, N, 1, N + 3)
            iteration(N - 1, 0, N - 2, 0, N, 1, N + 1, 1, None)
            if eng is nc.vector:
                eng.wait_ge(pvp_done, PBURST * N)
            if eng is nc.gpsimd:
                eng.wait_ge(pvv_done, VBURST * N)
            iteration(N, 1, N - 1, 0, N + 1, 1, N + 2, 1, None)
            iteration(N + 1, 1, N, 1, N + 2, 1, N + 3, 1, None)
            iteration(N + 2, 1, N + 1, 1, N + 3, 1, None, 1, None)
            iteration(N + 3, 1, N + 2, 1, None, 1, None, 1, None)
            c_unit(N + 3, 1)

        assert CHUNKS == 4 and BATCH == 2

        def qk_slot(ring, room, m, nb):
            S = len(ring)
            return room[m] if nb and m < S else ring[m % S]

        def pv_slot(ring, room, m, b):
            S = len(ring)
            return room[m % S] if b else ring[m % S]

        def qk_slot_free(eng, S, m, n, nb, qk_used, pv_used, other_qk_done):
            T = 2 * S
            if not nb:
                if m >= S:
                    eng.wait_ge(qk_used, T * n + m - S + 1)
                elif n == 1:
                    eng.wait_ge(qk_used, T * n + m - S + 1)
                elif n > 1:
                    eng.wait_ge(pv_used, T * (n - 1) + m - S + 1)
            elif n == CHUNKS and m < S:
                eng.wait_ge(other_qk_done, T_OTHER[S] * CHUNKS)
            elif n <= CHUNKS + 1 and m >= S:
                eng.wait_ge(pv_used, T * (n - 1) + m - 2 * S + 1)
            else:
                eng.wait_ge(qk_used, T * (n - 1) + m + 1)

        def pv_slot_free(eng, S, m, u, b, qk_used, pv_used):
            T = 2 * S
            if not b and m < S:
                eng.wait_ge(qk_used, T * (u + 2) + m - S + 1)
            else:
                eng.wait_ge(pv_used, T * u + m - S + 1)

        T_OTHER = {VSLOTS: PBURST, PSLOTS: VBURST}

        def a_base(u, b):
            return 8 * u + 4 * b

        def values_there(b):
            return a_base(CHUNKS * (b + 1), b) + 4

        block = ctx.enter_context(nc.Block())

        @block.sync
        def _(sp):
            def chunk_of(t, u):
                return t[u // CHUNKS, :, CT * (u % CHUNKS):CT * (u % CHUNKS) + CT, :]

            def load_xa(u):
                need(sp, xhatA_done, u)
                sp.dma_start(xa[:, :, :], chunk_of(x_v, u)).then_inc(xa_in, 16)

            def load_xb(u):
                if u < CHUNKS - 1:
                    need(sp, y2_read, 2 * u)
                else:
                    sp.wait_ge(y_read, 2 * u)
                sp.dma_start(xb[:, :, :], chunk_of(x_v, u)).then_inc(xb_in, 16)

            def store(u):
                sp.wait_ge(y2_read, 2 * u + 2)
                sp.dma_start(chunk_of(out_v, u), x2[:, :, :]).then_inc(out_done, 16)

            wmod_v = wmod.rearrange("(k p) n -> p k n", p=P)
            for dst, src in ((cT_sb[:, :, :], cT), (wmod_sb[:, :, 0:2 * D], wmod_v[:, :, 0:2 * D])):
                sp.dma_start(dst, src).then_inc(ld_mod, 16)
            load_xa(0)
            for dst, src in ((perm_sb[:, :, :], perm), (wqkv_sb[:, :, :], wqkv.rearrange("(k p) n -> p k n", p=P)),
                             (bqkv_sb[:, :], bqkv)):
                sp.dma_start(dst, src).then_inc(ld_qkv, 16)
            load_xa(1)
            sp.dma_start(wmod_sb[:, :, 2 * D:6 * D], wmod_v[:, :, 2 * D:6 * D]).then_inc(ld_rest, 16)
            for dst, src in ((wproj_sb, wproj.rearrange("(k p) n -> p k n", p=P)),
                             (wbase_sb, wbase.rearrange("(k p) n -> p k n", p=P)), (wup_sb, wup),
                             (bproj_sb, bproj.rearrange("(a n) -> a n", a=1).broadcast_to([P, D]))):
                sp.dma_start(dst, src).then_inc(ld_scaled, 16)
            load_xa(2)
            for dst, src in ((permT_sb[:, :, :], permT), (sel_sb[:, :, :], sel), (mask_sb[:, :], mask),
                             (maskrow_sb[:, :], maskrow),
                             (wdown_sb[:, :, :], wdown.rearrange("(k p) n -> p k n", p=P)),
                             (rb_sb[:, :], rb.rearrange("(a n) -> a n", a=1).broadcast_to([P, E])),
                             (lower_sb[:, :, :], lower)):
                sp.dma_start(dst, src).then_inc(ld_const, 16)
            load_xb(0)
            load_xa(3)
            load_xa(4)
            load_xa(5)
            for u in range(UNITS):
                if u + 6 < UNITS:
                    load_xa(u + 6)
                if u >= CHUNKS - 1:
                    load_xb(u)
                if u:
                    store(u - 1)
                if 0 < u < CHUNKS - 1:
                    load_xb(u)
            store(UNITS - 1)
            sp.wait_ge(out_done, 16 * UNITS)

        @block.gpsimd
        def _(pool):
            g = nc.gpsimd

            def scale_weights():
                pool.wait_ge(gates_done, 1)
                pool.wait_ge(ld_scaled, 64)
                for b in range(BATCH):
                    for k in range(HALVES):
                        g.tensor_tensor(wproj_s[b][:, k, :], wproj_sb[:, k, :], gates[:, b, 0, :], ALU.mult)\
                            .then_inc(scaled_done, 1)
                        g.tensor_tensor(wbase_s[b][:, k, :], wbase_sb[:, k, :], gates[:, b, 1, :], ALU.mult)\
                            .then_inc(scaled_done, 1)
                    g.tensor_tensor(wup_s[b][:, :], wup_sb, gates[0:NG + 1, b, 1, :], ALU.mult)\
                        .then_inc(scaled_done, 1)
                    g.tensor_tensor(brow[b][:, :], bproj_sb, gates[:, b, 0, :], ALU.mult)\
                        .then_inc(scaled_done, 1)
                pool.wait_ge(scaled_done, 12)

            def rstd(u, stats, step_sem, per, mv, ve, rst, bias, free, done):
                need(pool, done, 2 * u)
                need(pool, free, u)
                pool.wait_ge(stats, 2 * u + 2)
                link, count = steps(pool, step_sem, per * u)
                link(g.tensor_tensor(ve[:, 0, :], mv[:, 4, :], lnc[:, 0, :], ALU.add))
                link(g.tensor_tensor(ve[:, 1, :], ve[:, 0, :], lnc[:, 1, :], ALU.pow))
                link(g.tensor_tensor(ve[:, 2, :], mv[:, 0, :], ve[:, 1, :], ALU.mult))
                assert count[0] == per
                g.tensor_tensor(rst[:, :], ve[:, 1, :], lnc[:, 2, :], ALU.mult).then_inc(done, 1)
                g.tensor_tensor(bias[:, :], ve[:, 2, :], lnc[:, 3, :], ALU.mult).then_inc(done, 1)

            def rstd_a(u):
                rstd(u, statsA, pa_step, PA_STEPS, mvA, veA, rstdA, biasA, xhatA_done, rstdA_done)

            def rstd_c(u):
                rstd(u, statsC, pc_step, PC_STEPS, mvC, veC, rstdC, biasC, xhatC_done, rstdC_done)

            def qk_products(n, nb, half):
                pool.wait_ge(kpre_done, nb + 1)
                chunk = n - CHUNKS * nb
                for m in range(half * PSLOTS, (half + 1) * PSLOTS):
                    qk_slot_free(pool, PSLOTS, m, n, nb, qkp_used, pvp_used, qkv_done)
                    g.tensor_tensor(qk_slot(pring, kroom[VSLOTS:], m, nb).rearrange("p (h t) -> p h t", h=HALVES),
                                    queriesT[:, :, ds(CW * chunk, CW)],
                                    keysT[nb][:, :, ds(PRE * P - COLS[QK_P[m]] + CW * chunk, CW)], ALU.mult)\
                        .then_inc(qkp_done, 1)

            def pv_products(u, b, half):
                if half == 0:
                    pool.wait_ge(a_read, values_there(b))
                    pool.wait_ge(probs_done, u + 1)
                chunk = u - CHUNKS * b
                for m in range(half * PSLOTS, (half + 1) * PSLOTS):
                    k = PV_P[m]
                    pv_slot_free(pool, PSLOTS, m, u, b, qkp_used, pvp_used)
                    g.tensor_tensor(
                        pv_slot(pring, vroom[VSLOTS:], m, b).rearrange("p (a d) -> p a d", d=DH),
                        probs[:, k, :].unsqueeze(2).broadcast_to([P, CT * HEADS, DH]),
                        vals[b][:, ds((PRE - BACK[k]) * D + CT * D * chunk, CT * D)]
                        .rearrange("p (a d) -> p a d", d=DH), ALU.mult).then_inc(pvp_done, 1)

            def bias_x(u, b):
                pool.wait_ge(xb_in, 16 * u + 16)
                g.tensor_tensor(xb[:, :, :], xb[:, :, :], brow[b][:, :].unsqueeze(1).broadcast_to([P, CT, D]),
                                ALU.add).then_inc(xb_pre, 1)

            def a_unit(u, b):
                rstd_a(u + 1)

            def iteration(u, b, c, cb, n, nb, m, mb, a):
                if u is None:
                    scale_weights()
                    qk_products(n, nb, 0)
                if a is not None:
                    if c is not None:
                        rstd_c(c)
                    qk_products(n, nb, 1)
                    if u is not None:
                        pv_products(u, b, 0)
                    if a < UNITS - 1:
                        rstd_a(a + 1)
                    if u is not None:
                        pv_products(u, b, 1)
                else:
                    pv_products(u, b, 0)
                    rstd_c(c)
                    if m is not None:
                        qk_products(m, mb, 0)
                    pv_products(u, b, 1)
                    bias_x(u, b)
                if a is not None:
                    qk_products(m, mb, 0)
                if a is not None and u is not None:
                    bias_x(u, b)
                if m is not None and mb:
                    qk_products(m, mb, 1)

            for k, value in enumerate((D * EPS, -0.5, D ** 0.5, -0.5 * D ** 0.5)):
                g.memset(lnc[:, k, :], value).then_inc(const_done, 1)
            g.memset(lora[:, :, NG:NG + 1], 1.0).then_inc(const_done, 1)
            pool.wait_ge(const_done, 5)
            rstd_a(0)
            schedule(pool, a_unit, lambda: None, iteration, lambda u, b: rstd_c(u))

        @block.scalar
        def _(act):
            s = nc.scalar

            def normalise(u, x_buf, xhat, rst, bias, ready, done):
                act.wait_ge(ready, 2 * u + 2)
                for t in range(CT):
                    ins = s.activation(xhat[:, t, :], x_buf[:, t, :], ACT.Identity,
                                       bias=bias[:, t:t + 1], scale=rst[:, t:t + 1])
                ins.then_inc(done, 1)

            def normalise_a(u, before):
                need(act, a_full, before)
                normalise(u, xa, xhatA, rstdA, biasA, rstdA_done, xhatA_done)

            def normalise_c(u, x_buf):
                need(act, out_done, 16 * u)
                need(act, h2T_full, 2 * u)
                normalise(u, x_buf, xhatC, rstdC, biasC, rstdC_done, xhatC_done)

            def evac_a(u, b, group, dst, bank_n, func=ACT.Identity, **kw):
                act.wait_ge(a_full, a_base(u, b) + group + 1)
                s.activation(dst, pA[bank_n][:, :], func, **kw).then_inc(a_read, 1)

            def hT_halves(a, ab):
                for k in range(HALVES):
                    evac_a(a, ab, k, hT[:, k, :], k, bias=modT[:, 0, k, ab:ab + 1],
                           scale=modT[:, 1, k, ab:ab + 1])

            def keys(a, ab):
                for k in range(HALVES):
                    evac_a(a, ab, 2 + k, keysT[ab][:, k, ds(PRE * P + CW * (a - CHUNKS * ab), CW)], k,
                           bias=bqkv_sb[:, 2 + k:3 + k])

            def queries(a, ab):
                if ab:
                    act.wait_ge(qkv_done, VBURST * (a - CHUNKS + 1))
                    act.wait_ge(qkp_done, PBURST * (a - CHUNKS + 1))
                for k in range(HALVES):
                    evac_a(a, ab, 6 + k, queriesT[:, k, ds(CW * (a - CHUNKS * ab), CW)], k,
                           bias=bqkv_sb[:, k:k + 1])

            def values(a, ab, n):
                evac_a(a, ab, 4 + n, vals[ab][:, ds((PRE + 2 * n) * D + CT * D * (a - CHUNKS * ab), 2 * D)], n,
                       ACT.Copy)

            def prefix_keys(b):
                act.wait_ge(a_read, a_base(CHUNKS * (b + 1) - 1, b) + 4)
                s.activation(keysT[b][:, :, 0:PRE * P], keysT[b][:, :, (TILES * P - 1):(TILES + PRE) * P - 1],
                             ACT.Copy).then_inc(kpre_done, 1)

            def prefix_values(b):
                for n in range(4):
                    act.wait_ge(a_full, a_base(CHUNKS * (b + 1), b) + n + 1)
                    s.activation(vals[b][:, 2 * n * D:2 * (n + 1) * D], pA[n % 2][:, :], ACT.Copy)\
                        .then_inc(a_read, 1)

            def scores_out(n):
                act.wait_ge(qkv_used, VBURST * (n + 1))
                act.wait_ge(qkp_used, PBURST * (n + 1))
                for k in range(HALVES):
                    s.activation(scoresT[:, k, :], pS[k][0:ND * HH, :], ACT.Copy).then_inc(sT_read, 1)

            def exponentials(u):
                act.wait_ge(ssub_done, u + 1)
                s.activation(probs[:, :, :], probs[:, :, :], ACT.Exp, scale=SCALE).then_inc(exp_done, 1)

            def h2T_halves(c, cb):
                for k in range(HALVES):
                    act.wait_ge(h2T_full, 2 * c + k + 1)
                    s.activation(h2T[:, k, :], pB[k][:, :], ACT.Identity, bias=modT[:, 2, k, cb:cb + 1],
                                 scale=modT[:, 3, k, cb:cb + 1]).then_inc(h2T_read, 1)

            def router_exp(c):
                act.wait_ge(lsub_done, c + 1)
                s.activation(lexp[:, :, :], lsub[:, :, :], ACT.Exp).then_inc(lexp_done, 1)

            def lora_out(c):
                act.wait_ge(loraT_full, c + 1)
                s.activation(loraT[:, :], pB[1][0:NG + 1, :], ACT.Copy).then_inc(loraT_read, 1)

            def attention_out(u):
                act.wait_ge(pvv_used, VBURST * (u + 1))
                act.wait_ge(pvp_used, PBURST * (u + 1))
                for k in range(HALVES):
                    s.activation(attnT[:, k, :], pO[k][:, :], ACT.Identity,
                                 bias=bqkv_sb[:, 4 + k:5 + k]).then_inc(attnT_read, 1)

            def shifted_probs(n):
                act.wait_ge(pshift_full, n + 1)
                need(act, pvv_done, VBURST * n)
                s.activation(shifted[:, :, :].rearrange("p k g -> p (k g)"), pA[1][:, 0:NSH * CT * HEADS],
                             ACT.Copy).then_inc(shifted_done, 1)

            def a_unit(u, b):
                hT_halves(u, b)
                keys(u, b)
                normalise_a(u + 1, a_base(u, b) + 2)
                values(u, b, 0)
                values(u, b, 1)
                queries(u, b)

            def iteration(u, b, c, cb, n, nb, m, mb, a):
                if u is None:
                    prefix_keys(0)
                    prefix_values(0)
                    act.wait_ge(modT_done, 4)
                    act.wait_ge(scaled_done, 12)
                if a is not None:
                    hT_halves(a, 1)
                    if c is not None:
                        normalise_c(c, xb)
                    keys(a, 1)
                    scores_out(n)
                    if c is not None:
                        h2T_halves(c, cb)
                    values(a, 1, 0)
                    if c is not None:
                        router_exp(c)
                    values(a, 1, 1)
                    if a == UNITS - 1:
                        prefix_keys(1)
                    else:
                        normalise_a(a + 1, a_base(a, 1) + 2)
                    if c is not None:
                        lora_out(c)
                    if u is not None:
                        attention_out(u)
                    exponentials(n)
                    queries(a, 1)
                else:
                    normalise_c(c, xr)
                    if n is not None:
                        scores_out(n)
                    if u == CHUNKS - 1:
                        prefix_values(1)
                    h2T_halves(c, cb)
                    router_exp(c)
                    lora_out(c)
                    if n is not None:
                        exponentials(n)
                    attention_out(u)
                if n is not None:
                    shifted_probs(n)

            def c_unit(c, cb):
                normalise_c(c, xr)
                h2T_halves(c, cb)
                router_exp(c)
                lora_out(c)

            act.wait_ge(ld_mod, 32)
            s.activation(silu[:, 0, :, :], cT_sb[:, :, :], ACT.Exp, scale=-1.0).then_inc(expc_done, 1)
            normalise_a(0, 0)
            act.wait_ge(modT_done, 2)
            act.wait_ge(ld_qkv, 48)
            schedule(act, a_unit, lambda: None, iteration, c_unit)

        @block.vector
        def _(dve):
            v = nc.vector

            def modulation():
                link, _ = steps(dve, setup_v, 0)
                dve.wait_ge(expc_done, 1)
                link(v.tensor_scalar(silu[:, 1, :, :], silu[:, 0, :, :], 1.0, None, ALU.add))
                link(v.reciprocal(silu[:, 2, :, :], silu[:, 1, :, :]))
                link(v.tensor_tensor(silu[:, 0, :, :], cT_sb[:, :, :], silu[:, 2, :, :], ALU.mult))
                v.tensor_copy(silub, silu[:, 0, :, :].unsqueeze(3).broadcast_to([P, HALVES, BATCH, P]))\
                    .then_inc(silu_done, 1)

            def shift_scale(v_):
                dve.wait_ge(mod_full, v_ + 1)
                src = pO[0][:, 8 * v_:8 * v_ + 8].rearrange("p (s k b) -> p s k b", s=2, k=HALVES)
                v.tensor_copy(modT[:, 2 * v_, :, :], src[:, 0, :, :]).then_inc(modT_done, 1)
                v.tensor_scalar(modT[:, 2 * v_ + 1, :, :], src[:, 1, :, :], 1.0, None, ALU.add)\
                    .then_inc(modT_done, 1)

            def gate_rows():
                link, _ = steps(dve, setup_v, 3)
                for b in range(BATCH):
                    src = pS[b][:, :].rearrange("p (v n) -> p v n", v=2)
                    link(v.tensor_scalar(gsign[:, b, :, :], src, 0.0, 2.0, ALU.is_ge, ALU.mult))
                    link(v.scalar_tensor_tensor(gates[:, b, :, :], gsign[:, b, :, :], -1.0, src, ALU.add,
                                                ALU.mult))
                    link(v.tensor_scalar(gates[:, b, :, :], gates[:, b, :, :], 0.25, None, ALU.max))
                v.scalar_tensor_tensor(gates, gsign, -1.0, gates, ALU.add, ALU.mult).then_inc(gates_done, 1)

            def stats(u, x_buf, bn, mv, step_sem, base, free, done):
                need(dve, free, 2 * u)
                for t in range(CT):
                    v.bn_stats(bn[:, t, :], x_buf[:, t, :]).then_inc(step_sem, 1)
                dve.wait_ge(step_sem, base + CT)
                v.tensor_tensor(mv[:, 0, :], bn[:, :, 1], bn[:, :, 4], ALU.add).then_inc(done, 1)
                v.tensor_tensor(mv[:, 1, :], bn[:, :, 2], bn[:, :, 5], ALU.add).then_inc(step_sem, 1)
                v.tensor_tensor(mv[:, 2, :], bn[:, :, 1], bn[:, :, 4], ALU.subtract).then_inc(step_sem, 1)
                dve.wait_ge(step_sem, base + CT + 2)
                v.scalar_tensor_tensor(mv[:, 3, :], mv[:, 2, :], D / 4, mv[:, 2, :], ALU.mult, ALU.mult)\
                    .then_inc(step_sem, 1)
                dve.wait_ge(step_sem, base + CT + 3)
                v.tensor_tensor(mv[:, 4, :], mv[:, 1, :], mv[:, 3, :], ALU.add).then_inc(done, 1)

            def stats_a(u):
                dve.wait_ge(xa_in, 16 * u + 16)
                stats(u, xa, bnA, mvA, va_step, VA_STEPS * u, rstdA_done, statsA)

            def residual_a(u, bank, x_buf):
                dve.wait_ge(xb_pre, u + 1)
                need(dve, y2_read, 2 * u)
                for n in range(2):
                    dve.wait_ge(y_full, 2 * u + n + 1)
                    v.tensor_tensor(x_buf[:, 2 * n:2 * n + 2, :], bank[n][:, :].rearrange("p (t c) -> p t c", c=D),
                                    xb[:, 2 * n:2 * n + 2, :], ALU.add).then_inc(y_read, 1)
                dve.wait_ge(y_read, 2 * u + 2)
                stats(u, x_buf, bnC, mvC, vc_step, VC_STEPS * u, rstdC_done, statsC)

            def qk_products(n, nb, half):
                dve.wait_ge(kpre_done, nb + 1)
                chunk = n - CHUNKS * nb
                for m in range(half * VSLOTS, (half + 1) * VSLOTS):
                    qk_slot_free(dve, VSLOTS, m, n, nb, qkv_used, pvv_used, qkp_done)
                    v.tensor_tensor(qk_slot(vring, kroom, m, nb).rearrange("p (h t) -> p h t", h=HALVES),
                                    queriesT[:, :, ds(CW * chunk, CW)],
                                    keysT[nb][:, :, ds(PRE * P - COLS[QK_V[m]] + CW * chunk, CW)], ALU.mult)\
                        .then_inc(qkv_done, 1)

            def pv_products(u, b, half):
                if half == 0:
                    dve.wait_ge(a_read, values_there(b))
                chunk = u - CHUNKS * b
                for m in range(half * VSLOTS, (half + 1) * VSLOTS):
                    k = PV_V[m]
                    pv_slot_free(dve, VSLOTS, m, u, b, qkv_used, pvv_used)
                    if k == 1:
                        dve.wait_ge(shifted_done, u + 1)
                    pr = probs[:, k, :] if k == 0 else shifted[:, k - 1, :]
                    v.tensor_tensor(
                        pv_slot(vring, vroom, m, b).rearrange("p (a d) -> p a d", d=DH),
                        pr.unsqueeze(2).broadcast_to([P, CT * HEADS, DH]),
                        vals[b][:, ds((PRE - BACK[k]) * D + CT * D * chunk, CT * D)]
                        .rearrange("p (a d) -> p a d", d=DH), ALU.mult).then_inc(pvv_done, 1)

            def softmax_front(u):
                need(dve, pvp_done, PBURST * u)
                need(dve, pshift_full, u)
                G = 2 * HALVES
                link, count = steps(dve, vb_step, VB_STEPS * u)
                for n in range(2):
                    dve.wait_ge(stok_full, 2 * u + n + 1)
                    sc = pS[n][:, 0:G * ND * HH].rearrange("p (g o h) -> p g o h", g=G, o=ND)
                    mx = smax[:, n * 32:n * 32 + 32].rearrange("p (g h) -> p g h", h=HH)
                    link(v.tensor_reduce(mx, sc.rearrange("p g o h -> p g h o"), AX.X, ALU.max))
                    ins = v.tensor_tensor(
                        probs[:, :, n * 32:n * 32 + 32].rearrange("p o (g h) -> p g o h", h=HH), sc,
                        mx.unsqueeze(2).broadcast_to([P, G, ND, HH]), ALU.subtract)
                ins.then_inc(ssub_done, 1)
                assert count[0] == 2

            def softmax_back(u):
                link, count = steps(dve, vb_step, VB_STEPS * u + 2)
                dve.wait_ge(exp_done, u + 1)
                link(v.tensor_reduce(ssum[:, :], probs[:, :, :].rearrange("p o g -> p g o"), AX.X, ALU.add))
                link(v.reciprocal(srec[:, :], ssum[:, :]))
                v.tensor_tensor(probs[:, :, :], probs[:, :, :],
                                srec[:, :].unsqueeze(1).broadcast_to([P, ND, CT * HEADS]), ALU.mult)\
                    .then_inc(probs_done, 1)
                dve.wait_ge(probs_done, u + 1)
                assert count[0] == 2

            def router(u):
                link, count = steps(dve, vc_step, VC_STEPS * u + CT + 3)
                dve.wait_ge(down_full, u + 1)
                down = pB[0][:, 0:CT * NA].rearrange("p (t n) -> p t n", n=NA)
                link(v.tensor_tensor(lg[:, :, :], down[:, :, NG:NA],
                                     rb_sb[:, :].unsqueeze(1).broadcast_to([P, CT, E]), ALU.add))
                link(v.tensor_reduce(lmax[:, :], lg[:, :, :], AX.X, ALU.max))
                v.tensor_tensor(lsub[:, :, :], lg[:, :, :], lmax[:, :].unsqueeze(2).broadcast_to([P, CT, E]),
                                ALU.subtract).then_inc(lsub_done, 1)
                other = lg[:, :, :].unsqueeze(2).broadcast_to([P, CT, E, E])
                own = lg[:, :, :].unsqueeze(3).broadcast_to([P, CT, E, E])
                link(v.tensor_tensor(level[:, :, :, :], other, own, ALU.is_ge))
                link(v.tensor_tensor(above[:, :, :, :], other, own, ALU.is_gt))
                link(v.tensor_tensor(level[:, :, :, :], level[:, :, :, :],
                                     lower_sb[:, :, :].unsqueeze(1).broadcast_to([P, CT, E, E]), ALU.mult))
                link(v.tensor_tensor(above[:, :, :, :], above[:, :, :, :], level[:, :, :, :], ALU.max))
                link(v.tensor_reduce(rank[:, :, :], above[:, :, :, :], AX.X, ALU.add))
                dve.wait_ge(lexp_done, u + 1)
                link(v.scalar_tensor_tensor(picked[:, :, :], rank[:, :, :], TOPK - 0.5, lexp[:, :, :],
                                            ALU.is_lt, ALU.mult))
                link(v.tensor_reduce(zall[:, :], lexp[:, :, :], AX.X, ALU.add))
                link(v.tensor_reduce(zpick[:, :], picked[:, :, :], AX.X, ALU.add))
                link(v.scalar_tensor_tensor(zall[:, :], zall[:, :], 1e-6, zpick[:, :], ALU.mult, ALU.add))
                link(v.reciprocal(zrec[:, :], zall[:, :]))
                link(v.tensor_tensor(wsel[:, :, :], picked[:, :, :],
                                     zrec[:, :].unsqueeze(2).broadcast_to([P, CT, E]), ALU.mult))
                need(dve, loraT_full, u)
                v.tensor_tensor(lora[:, :, 0:NR].rearrange("p t (e r) -> p t e r", r=R),
                                down[:, :, 0:NR].rearrange("p t (e r) -> p t e r", r=R),
                                wsel[:, :, :].unsqueeze(3).broadcast_to([P, CT, E, R]), ALU.mult)\
                    .then_inc(lora_done, 1)
                v.tensor_copy(lora[:, :, NR:NG], down[:, :, NR:NG]).then_inc(lora_done, 1)
                assert count[0] == VC_STEPS - CT - 3

            def residual_c(u, x_buf):
                for n in range(2):
                    dve.wait_ge(y2_full, 2 * u + n + 1)
                    v.tensor_tensor(x2[:, 2 * n:2 * n + 2, :], pB[n][:, :].rearrange("p (t c) -> p t c", c=D),
                                    x_buf[:, 2 * n:2 * n + 2, :], ALU.add).then_inc(y2_read, 1)

            def a_unit(u, b):
                stats_a(u + 1)

            def iteration(u, b, c, cb, n, nb, m, mb, a):
                if u is None:
                    shift_scale(1)
                    gate_rows()
                    dve.wait_ge(gates_done, 1)
                    qk_products(n, nb, 0)
                if a is not None:
                    if c is not None:
                        residual_a(c, pB, xb)
                    qk_products(n, nb, 1)
                    if u is not None:
                        pv_products(u, b, 0)
                    if c is not None:
                        router(c)
                    if a < UNITS - 1:
                        stats_a(a + 1)
                    if u is not None:
                        pv_products(u, b, 1)
                    softmax_front(n)
                    softmax_back(n)
                    qk_products(m, mb, 0)
                    if c is not None:
                        residual_c(c, xb)
                    if mb:
                        qk_products(m, mb, 1)
                else:
                    residual_a(c, pB if c < CHUNKS - 1 else pA, xr)
                    pv_products(u, b, 0)
                    if m is not None:
                        qk_products(m, mb, 0)
                    router(c)
                    pv_products(u, b, 1)
                    if n is not None:
                        softmax_front(n)
                        softmax_back(n)
                    if m is not None:
                        qk_products(m, mb, 1)
                    residual_c(c, xr)

            def c_unit(c, cb):
                residual_a(c, pA, xr)
                router(c)
                residual_c(c, xr)

            modulation()
            stats_a(0)
            shift_scale(0)
            schedule(dve, a_unit, lambda: None, iteration, c_unit)

        @block.tensor
        def _(pe):
            t_ = nc.tensor
            ident = perm_sb[:, 0, :]

            def a_group(u, b, group):
                need(pe, a_read, a_base(u, b) + group - 1)
                if group == 1 and b and u > CHUNKS:
                    pe.wait_ge(shifted_done, u - CHUNKS)
                return pA[group % 2]

            def hT_transposes(a, ab):
                pe.wait_ge(xhatA_done, a + 1)
                for k in range(HALVES):
                    dst = a_group(a, ab, k)
                    for t in range(CT):
                        ins = t_.transpose(dst[:, t * P:(t + 1) * P], xhatA[:, t, k * P:(k + 1) * P], ident)
                    ins.then_inc(a_full, 1)

            def project_T(a, ab, group, col):
                dst = a_group(a, ab, group)
                for k in range(HALVES):
                    ins = t_.matmul(dst[:, :], wqkv_sb[:, k, col:col + P], hT[:, k, :], start=(k == 0),
                                    stop=(k == HALVES - 1))
                ins.then_inc(a_full, 1)

            def keys(a, ab):
                pe.wait_ge(a_read, a_base(a, ab) + 2)
                for k in range(HALVES):
                    project_T(a, ab, 2 + k, D + k * P)

            def queries(a, ab, k):
                project_T(a, ab, 6 + k, k * P)

            def values(a, ab, n):
                dst = a_group(a, ab, 4 + n)
                for t in range(2):
                    for k in range(HALVES):
                        col = (2 * n + t) * P
                        ins = t_.matmul(dst[:, t * D:(t + 1) * D], hT[:, k, col:col + P],
                                        wqkv_sb[:, k, 2 * D:3 * D], start=(k == 0), stop=(k == HALVES - 1))
                ins.then_inc(a_full, 1)

            def prefix_values(b):
                pe.wait_ge(a_read, a_base(CHUNKS * (b + 1), b))
                if b:
                    pe.wait_ge(shifted_done, CHUNKS)
                for n in range(4):
                    pe.wait_ge(a_read, a_base(CHUNKS * (b + 1), b) + n - 1)
                    at = (PRE + 8 + 2 * n) * D
                    t_.matmul(pA[n % 2][:, :], perm_sb[:, 1, :], vals[b][:, at:at + 2 * D], start=True,
                              stop=True).then_inc(a_full, 1)

            def scores(n, nb, rounds):
                chunk = n - CHUNKS * nb
                for r in rounds:
                    if r == 0:
                        need(pe, ssub_done, n)
                        for h in range(HALVES):
                            t_.matmul(pS[h][0:ND * HH, :], maskrow_sb[:, :], mask_sb[:, ds(CW * chunk, CW)],
                                      start=True, stop=False, skip_group_check=True)
                    nv, np_ = (sum(e == w for rr in QK_ROUNDS[:r + 1] for e, _ in rr) for w in "vp")
                    pe.wait_ge(qkv_done, VBURST * n + nv)
                    pe.wait_ge(qkp_done, PBURST * n + np_)
                    for h in range(HALVES):
                        for e, k in QK_ROUNDS[r]:
                            src = (qk_slot(vring, kroom, QK_V.index(k), nb) if e == "v" else
                                   qk_slot(pring, kroom[VSLOTS:], QK_P.index(k), nb))
                            q = k // 4
                            ins = t_.matmul(pS[h][32 * q:32 * q + 32, :], sel_sb[:, k % 4, :],
                                            src[:, h * CW:(h + 1) * CW], start=False, stop=(r == 3),
                                            skip_group_check=True)
                            if h == HALVES - 1:
                                ins.then_inc(qkv_used if e == "v" else qkp_used, 1)

            def score_transposes(n):
                pe.wait_ge(sT_read, 2 * n + 2)
                for t in range(CT):
                    for h in range(HALVES):
                        at = ((t % 2) * HALVES + h) * ND * HH
                        ins = t_.transpose(pS[t // 2][:, at:at + ND * HH], scoresT[:, h, t * P:(t + 1) * P],
                                           perm_sb[0:ND * HH, 0, 0:ND * HH])
                    if t % 2:
                        ins.then_inc(stok_full, 1)

            def shift_probs(n, a):
                if a is not None:
                    pe.wait_ge(a_read, a_base(a, 1) + 8)
                else:
                    pe.wait_ge(a_read, values_there(1))
                    pe.wait_ge(y_read, 2 * n - 2)
                pe.wait_ge(probs_done, n + 1)
                for k in range(1, 1 + NSH):
                    ins = t_.matmul(pA[1][:, (k - 1) * CT * HEADS:k * CT * HEADS], permT_sb[:, k - 1, :],
                                    probs[:, k, :], start=True, stop=True)
                ins.then_inc(pshift_full, 1)

            def attend(u, b, first, last):
                if first == 0:
                    need(pe, attnT_read, 2 * u)
                for i, (e, k) in list(enumerate(PV_ORDER))[first:last]:
                    if e == "v":
                        m = PV_V.index(k)
                        src = pv_slot(vring, vroom, m, b)
                        pe.wait_ge(pvv_done, VBURST * u + m + 1)
                    else:
                        m = PV_P.index(k)
                        src = pv_slot(pring, vroom[VSLOTS:], m, b)
                        pe.wait_ge(pvp_done, PBURST * u + m + 1)
                    place = perm_sb[:, PERMS.index(SHIFT[k]), :]
                    for t in range(CT):
                        for h in range(HALVES):
                            at = t * D + h * P
                            ins = t_.matmul(pO[h][:, t * P:(t + 1) * P], src[:, at:at + P], place,
                                            start=(i == 0 and t == 0), stop=(i == ND - 1),
                                            is_transpose=True, skip_group_check=True)
                    ins.then_inc(pvv_used if e == "v" else pvp_used, 1)

            def project(u, b, n_next, a):
                pe.wait_ge(attnT_read, 2 * u + 2)
                dst = pB
                if a is None:
                    dst = pA
                    pe.wait_ge(a_read, values_there(1))
                    pe.wait_ge(y_read, 2 * u)
                    if n_next is not None:
                        pe.wait_ge(shifted_done, n_next + 1)
                for n in range(2):
                    if a is not None:
                        need(pe, y2_read, 2 * u - 1 + n)
                    for t in range(2):
                        for k in range(HALVES):
                            col = (2 * n + t) * P
                            ins = t_.matmul(dst[n][:, t * D:(t + 1) * D], attnT[:, k, col:col + P],
                                            wproj_s[b][:, k, :], start=(k == 0), stop=(k == HALVES - 1))
                    ins.then_inc(y_full, 1)

            def h2T_transposes(c):
                pe.wait_ge(xhatC_done, c + 1)
                need(pe, y2_read, 2 * c)
                for k in range(HALVES):
                    pe.wait_ge(y_read, 2 * c + 1 + k)
                    for t in range(CT):
                        ins = t_.transpose(pB[k][:, t * P:(t + 1) * P], xhatC[:, t, k * P:(k + 1) * P], ident)
                    ins.then_inc(h2T_full, 1)

            def down(c):
                pe.wait_ge(h2T_read, 2 * c + 2)
                for t in range(CT):
                    for k in range(HALVES):
                        ins = t_.matmul(pB[0][:, t * NA:(t + 1) * NA], h2T[:, k, t * P:(t + 1) * P],
                                        wdown_sb[:, k, :], start=(k == 0), stop=(k == HALVES - 1))
                ins.then_inc(down_full, 1)

            def lora_transposes(c):
                pe.wait_ge(lora_done, 2 * c + 2)
                for t in range(CT):
                    ins = t_.transpose(pB[1][0:NG + 1, t * P:(t + 1) * P], lora[:, t, :], ident)
                ins.then_inc(loraT_full, 1)

            def up(c, cb):
                pe.wait_ge(loraT_read, c + 1)
                for n in range(2):
                    for t in range(2):
                        col = (2 * n + t) * P
                        dst = pB[n][:, t * D:(t + 1) * D]
                        for k in range(HALVES):
                            t_.matmul(dst, h2T[:, k, col:col + P], wbase_s[cb][:, k, :], start=(k == 0),
                                      stop=False)
                        ins = t_.matmul(dst, loraT[:, col:col + P], wup_s[cb][:, :], start=False, stop=True)
                    ins.then_inc(y2_full, 1)

            def a_unit(u, b):
                hT_transposes(u, b)
                keys(u, b)
                values(u, b, 0)
                values(u, b, 1)
                queries(u, b, 0)
                queries(u, b, 1)

            def iteration(u, b, c, cb, n, nb, m, mb, a):
                if u is None:
                    prefix_values(0)
                    pe.wait_ge(ld_const, 16 * 7)
                    pe.wait_ge(gates_done, 1)
                    pe.wait_ge(const_done, 5)
                    pe.wait_ge(scaled_done, 12)
                if a is not None:
                    scores(n, nb, [0, 1])
                    hT_transposes(a, 1)
                    keys(a, 1)
                    scores(n, nb, [2, 3])
                    if c is not None:
                        h2T_transposes(c)
                    values(a, 1, 0)
                    if c is not None:
                        down(c)
                    score_transposes(n)
                    values(a, 1, 1)
                else:
                    if n is not None:
                        scores(n, nb, range(4))
                    if u == CHUNKS - 1:
                        prefix_values(1)
                    h2T_transposes(c)
                    down(c)
                    if n is not None:
                        score_transposes(n)
                if u is not None:
                    attend(u, b, 0, 8)
                if c is not None:
                    lora_transposes(c)
                if u is not None:
                    attend(u, b, 8, ND)
                if a is not None:
                    queries(a, 1, 0)
                if c is not None:
                    up(c, cb)
                if a is not None:
                    queries(a, 1, 1)
                if n is not None:
                    shift_probs(n, a)
                if u is not None:
                    project(u, b, n, a)

            def c_unit(c, cb):
                h2T_transposes(c)
                down(c)
                lora_transposes(c)
                up(c, cb)

            def shift_scale(v_):
                for n in range(2):
                    for h in range(HALVES):
                        at = ((2 * v_ + n) * HALVES + h) * BATCH
                        for k in range(HALVES):
                            col = (3 * v_ + n) * D + h * P
                            ins = t_.matmul(pO[0][:, at:at + BATCH], wmod_sb[:, k, col:col + P],
                                            silu[:, 0, k, :], start=(k == 0), stop=(k == 1))
                ins.then_inc(mod_full, 1)

            def setup():
                pe.wait_ge(ld_rest, 16)
                for b in range(BATCH):
                    for n, vec in enumerate((2, 5)):
                        for k in range(HALVES):
                            t_.matmul(pS[b][:, n * D:(n + 1) * D], silub[:, k, b, :],
                                      wmod_sb[:, k, vec * D:(vec + 1) * D], start=(k == 0), stop=(k == 1))
                pe.wait_ge(modT_done, 2)
                shift_scale(1)

            pe.wait_ge(silu_done, 1)
            pe.wait_ge(ld_mod, 32)
            shift_scale(0)
            pe.wait_ge(ld_qkv, 48)
            schedule(pe, a_unit, setup, iteration, c_unit)


def kernel(**inputs):
    import numpy as np
    import concourse.bacc as bacc
    from ml_dtypes import bfloat16 as bf16
    from concourse.bass_utils import run_bass_kernel_spmd

    f = {k.replace("L0_attn_", "").replace("L0_ffn_", "").replace("L0_", ""): np.ascontiguousarray(v)
         for k, v in inputs.items()}
    perm = np.zeros((P, len(PERMS), P), np.float32)
    for n, m in enumerate(PERMS):
        perm[np.arange(P), n, (np.arange(P) + m) % P] = 1.0
    permT = np.zeros((P, NSH, P), np.float32)
    for n in range(NSH):
        permT[(np.arange(P) + SHIFT[1 + n]) % P, n, np.arange(P)] = 1.0
    sel = np.zeros((P, 4, 32), np.float32)
    for n in range(4):
        sel[np.arange(P), n, n * HH + np.arange(P) // DH] = 1.0
    token = (np.arange(TILES)[:, None] + TILES * np.arange(P)[None, :]).reshape(-1)
    mask = np.where(token[None, :] < np.array(DIST)[:, None], MASKED, 0.0).astype(bf16)
    maskrow = (np.arange(ND)[:, None] == np.arange(ND * HH)[None, :] // HH).astype(bf16)
    lower = np.broadcast_to((np.arange(E)[None, :] < np.arange(E)[:, None]).astype(np.float32), (P, E, E))
    arrays = {
        "x": f["x"],
        "cT": f["c"].T.reshape(HALVES, P, BATCH).transpose(1, 0, 2),
        "wmod": f["wmod"],
        "wqkv": f["W_qkv"],
        "bqkv": f["b_qkv"].reshape(3 * HALVES, P).T,
        "wproj": f["W_proj"],
        "bproj": f["b_proj"],
        "wbase": f["base_W"].T,
        "wdown": np.concatenate([f["routed_A"].reshape(NR, D), f["shared_A"], f["router_W"]]).T,
        "wup": np.concatenate([f["routed_B"].transpose(0, 2, 1).reshape(NR, D), f["shared_B"].T,
                               f["base_b"][None, :]]),
        "rb": f["router_b"],
        "perm": perm, "permT": permT, "sel": sel, "mask": mask, "maskrow": maskrow, "lower": lower,
    }
    arrays = {f"in_{k}": np.ascontiguousarray(a) for k, a in arrays.items()}
    nc = bacc.Bacc("TRN2", target_bir_lowering=False, num_devices=1)
    args = [nc.dram_tensor(k, a.shape, mybir.dt.from_np(a.dtype), kind="ExternalInput").ap()
            for k, a in arrays.items()]
    args.append(nc.dram_tensor("out", f["x"].shape, F32, kind="ExternalOutput").ap())
    build(nc, *args)
    r = run_bass_kernel_spmd(nc, [arrays], core_ids=[0])
    return r.results[0]["out"]
```

```python
from contextlib import ExitStack

import concourse.bass as bass
from concourse import mybir

F32 = mybir.dt.float32
BF16 = mybir.dt.bfloat16
ALU = mybir.AluOpType
ACT = mybir.ActivationFunctionType
AX = mybir.AxisListType

P = 128
BATCH, SEQ, D = 2, 2048, 256
HEADS, DH = 16, 16
HALVES = D // P
HH = HEADS // HALVES
TILES = SEQ // P
CT = 4
CHUNKS = TILES // CT
CW = CT * P
UNITS = BATCH * CHUNKS
PRE = 8
E, R, TOPK = 6, 16, 2
NR = E * R
NG = NR + R
NA = NG + E
SCALE = DH ** -0.5
EPS = 1e-5
MASKED = -1e30

DIST = [0, 16, 32, 64, 128, 256, 512, 1024, 1, 2, 4, 8]
ND = len(DIST)
SHIFT = [d // 16 for d in DIST]
BACK = [d if d < 16 else 0 for d in DIST]
COLS = [d * P if d < 16 else d // 16 for d in DIST]
NSH = 7

QK_ROUNDS = [("p", (8, 10)), ("v", (0, 4)), ("v", (1, 5)), ("v", (2, 6)), ("v", (3, 7)), ("p", (9, 11))]
PV_ORDER = [[("v", 0), ("p", (8, 9)), ("v", 1), ("v", 2), ("v", 3), ("v", 4), ("v", 5), ("v", 6), ("p", (10, 11)),
             ("v", 7)],
            [("p", (0,)), ("v", 1), ("p", (8,)), ("v", 2), ("v", 3), ("v", 4), ("p", (9,)), ("v", 5), ("v", 6),
             ("p", (10,)), ("v", 7), ("p", (11,))]]
QK_V = [k for e, ks in QK_ROUNDS if e == "v" for k in ks]
QK_P = [k for e, ks in QK_ROUNDS if e == "p" for k in ks]
PV_V = [[k for e, k in order if e == "v"] for order in PV_ORDER]
PV_P = [[ks for e, ks in order if e == "p"] for order in PV_ORDER]
VSLOTS, PSLOTS = 4, 2
VBURST, PBURST = 2 * VSLOTS, 2 * PSLOTS
assert len(QK_V) == len(PV_V[0]) == VBURST and len(QK_P) == PBURST
PAIRS, SINGLES = len(PV_P[0]), len(PV_P[1])
assert PAIRS == PSLOTS == 2 and all(SHIFT[k] == 0 for ks in PV_P[0] for k in ks)

VA_STEPS, VB_STEPS, VC_STEPS, VR_STEPS = 7, 5, 7, 13
PA_STEPS, PC_STEPS = 3, 3


def ds(start, size):
    return bass.ds(start, size)


def build(nc, x, cT, wmod, wqkv, bqkv, wproj, bproj, wbase, wdown, wup, rb, circ, sel, mask, maskrow,
          lower, out):
    x_v = x.rearrange("b (p j) c -> b p j c", j=TILES)
    out_v = out.rearrange("b (p j) c -> b p j c", j=TILES)

    with ExitStack() as ctx:
        def sb(name, shape, dt=F32):
            return ctx.enter_context(nc.sbuf_tensor(name, shape, dt))

        def bank(name):
            return ctx.enter_context(nc.psum_tensor(name, [P, 512], F32))

        def sem(name):
            return ctx.enter_context(nc.semaphore(name))

        KW = (PRE + TILES) * P
        keysT = [sb(f"keysT{b}", [P, HALVES, KW]) for b in range(BATCH)]
        vals = [sb(f"vals{b}", [P, (PRE + TILES) * D]) for b in range(BATCH)]
        queriesT = sb("queriesT", [P, HALVES, SEQ])
        vring = [sb(f"vprod{s}", [P, 2 * CW]) for s in range(VSLOTS)]
        pring = [sb(f"pprod{s}", [P, 2 * CW])[:, :] for s in range(PSLOTS)]
        xa = sb("xa", [P, CT, D])
        xb = sb("xb", [P, CT, D])
        xr = sb("xr", [P, CT, D])
        xhatA = sb("xhatA", [P, CT, D])
        hT = sb("hT", [P, HALVES, CW])
        x2 = sb("x2", [P, CT, D])
        h2T = sb("h2T", [P, HALVES, CW])
        probs = sb("probs", [P, ND, CT * HEADS])
        shifted = sb("shifted", [P, NSH, CT * HEADS])
        attnT = sb("attnT", [P, HALVES, CW])
        scoresT = attnT
        smax = sb("smax", [P, CT * HEADS])
        ssum = sb("ssum", [P, CT * HEADS])
        srec = sb("srec", [P, CT * HEADS])
        bnA = sb("bnA", [P, CT, 6])
        mvA = sb("mvA", [P, 5, CT])
        bnC = sb("bnC", [P, CT, 6])
        mvC = sb("mvC", [P, 5, CT])
        veA = sb("veA", [P, 3, CT])
        veC = sb("veC", [P, 3, CT])
        rstdA = sb("rstdA", [P, CT])
        rstdC = sb("rstdC", [P, CT])
        biasA = sb("biasA", [P, CT])
        biasC = sb("biasC", [P, CT])
        lnc = sb("lnc", [P, 4, CT])
        lg = sb("lg", [P, CT, E])
        lmax = sb("lmax", [P, CT])
        lsub = sb("lsub", [P, CT, E])
        lexp = sb("lexp", [P, CT, E])
        above = sb("above", [P, CT, E, E])
        level = sb("level", [P, CT, E, E])
        rank = sb("rank", [P, CT, E])
        picked = sb("picked", [P, CT, E])
        zall = sb("zall", [P, CT])
        zpick = sb("zpick", [P, CT])
        zrec = sb("zrec", [P, CT])
        wsel = sb("wsel", [P, CT, E])
        lora = sb("lora", [P, CT, NG + 1])
        loraT = sb("loraT", [NG + 1, CW])
        wqkv_sb = sb("wqkv_sb", [P, HALVES, 3 * D])
        bqkv_sb = sb("bqkv_sb", [P, 3 * HALVES])
        wdown_sb = sb("wdown_sb", [P, HALVES, NA])
        wproj_s = [sb(f"wproj_s{b}", [P, HALVES, D]) for b in range(BATCH)]
        wbase_s = [sb(f"wbase_s{b}", [P, HALVES, D]) for b in range(BATCH)]
        wup_s = [sb(f"wup_s{b}", [NG + 1, D]) for b in range(BATCH)]
        brow = [sb(f"brow{b}", [P, D]) for b in range(BATCH)]
        rb_sb = sb("rb_sb", [P, E])
        lower_sb = sb("lower_sb", [P, E, E])
        circ_sb = sb("circ_sb", [P, 2 * P])
        sel_sb = sb("sel_sb", [P, 4, 32])
        mask_sb = sb("mask_sb", [ND, SEQ], BF16)
        maskrow_sb = sb("maskrow_sb", [ND, 2, P], BF16)
        cT_sb = sb("cT_sb", [P, HALVES, BATCH])
        silu = sb("silu", [P, 3, HALVES, BATCH])
        modT = sb("modT", [P, 4, HALVES, BATCH])
        room = vals[1]
        wmod_sb = room[:, 0:2 * 6 * D].rearrange("p (k n) -> p k n", k=HALVES)
        at = 2 * 6 * D
        wproj_sb = room[:, at:at + 2 * D].rearrange("p (k n) -> p k n", k=HALVES)
        at += 2 * D
        wbase_sb = room[:, at:at + 2 * D].rearrange("p (k n) -> p k n", k=HALVES)
        at += 2 * D
        wup_sb = room[0:NG + 1, at:at + D]
        at += D
        bproj_sb = room[:, at:at + D]
        at += D
        gates = room[:, at:at + 4 * D].rearrange("p (b v n) -> p b v n", b=BATCH, v=2)
        gsign = vring[0][:, :].rearrange("p (b v n) -> p b v n", b=BATCH, v=2)
        silub = vring[1][:, 0:4 * P].rearrange("p (k b n) -> p k b n", k=HALVES, b=BATCH)

        PROD = 2 * CW
        first_keys = keysT[0][:, :, :].rearrange("p k n -> p (k n)")
        kroom = [first_keys[:, s * PROD:(s + 1) * PROD] for s in range(VSLOTS + PSLOTS)]
        vroom = [vals[0][:, s * PROD:(s + 1) * PROD] for s in range(VSLOTS + PSLOTS)]

        LAST = UNITS - 1
        hT_rows = hT[:, :, :].rearrange("p k (t c) -> p (k t) c", c=D)

        def x_of(c):
            return xr if c < CHUNKS - 2 else xa if c % 2 else hT_rows

        def xhatC_of(c):
            return xhatA if c >= CHUNKS - 1 and c % 2 else x2

        def outC_of(c):
            odd = c >= CHUNKS - 1 and c % 2
            return (outa_done if odd else out2_done), sum(xhatC_of(i) is xhatC_of(c) for i in range(c))

        def h2T_of(c):
            return queriesT[:, :, 0:CW] if c == LAST else h2T

        pS = [bank("pS0"), bank("pS1")]
        pO = [bank("pO0"), bank("pO1")]
        pB = [bank("pB0"), bank("pB1")]
        pA = [bank("pA0"), bank("pA1")]

        def downC(c):
            return pS if c == LAST else pB

        def sumC(c):
            return pA if c == LAST else pB

        ld_mod, ld_rest, ld_qkv, ld_const, ld_scaled = (sem(n) for n in
                                                         ("ld_mod", "ld_rest", "ld_qkv", "ld_const", "ld_scaled"))
        xa_in, xb_in, out2_done, outa_done = (sem(n) for n in ("xa_in", "xb_in", "out2_done", "outa_done"))
        expc_done, silu_done, mod_full, modT_done, gates_done, scaled_done = (
            sem(n) for n in ("expc_done", "silu_done", "mod_full", "modT_done", "gates_done", "scaled_done"))
        ld_circ = sem("ld_circ")
        const_done, setup_v = sem("const_done"), sem("setup_v")
        statsA, rstdA_done, xhatA_done = sem("statsA"), sem("rstdA_done"), sem("xhatA_done")
        statsC, rstdC_done, xhatC_done = sem("statsC"), sem("rstdC_done"), sem("xhatC_done")
        a_full, a_read = sem("a_full"), sem("a_read")
        kpre_done, vpre_in = sem("kpre_done"), sem("vpre_in")
        qkv_done, qkp_done, pvv_done, pvp_done = (sem(n) for n in ("qkv_done", "qkp_done", "pvv_done", "pvp_done"))
        qkv_used, qkp_used, pvv_used, pvp_used = (sem(n) for n in ("qkv_used", "qkp_used", "pvv_used", "pvp_used"))
        sT_read, y2_out = sem("sT_read"), sem("y2_out")
        stok_full, ssub_done, exp_done, probs_done = (sem(n) for n in
                                                      ("stok_full", "ssub_done", "exp_done", "probs_done"))
        pshift_full, shifted_done, attnT_read = sem("pshift_full"), sem("shifted_done"), sem("attnT_read")
        xb_pre, y_full, y_read = sem("xb_pre"), sem("y_full"), sem("y_read")
        h2T_full, h2T_read = sem("h2T_full"), sem("h2T_read")
        down_full, lsub_done, lexp_done, lora_done = (sem(n) for n in
                                                      ("down_full", "lsub_done", "lexp_done", "lora_done"))
        loraT_full, loraT_read, y2_full, y2_read = (sem(n) for n in
                                                    ("loraT_full", "loraT_read", "y2_full", "y2_read"))
        va_step, vb_step, vc_step, vr_step = (sem(n) for n in ("va_step", "vb_step", "vc_step", "vr_step"))
        pa_step, pc_step, pair_step = sem("pa_step"), sem("pc_step"), sem("pair_step")

        def need(eng, s, value):
            if not isinstance(value, int) or value > 0:
                eng.wait_ge(s, value)

        def steps(eng, s, base):
            count = [0]

            def link(ins):
                count[0] += 1
                ins.then_inc(s, 1)
                eng.wait_ge(s, base + count[0])
            return link, count

        def schedule(eng, a_unit, setup, iteration):
            setup()
            a_unit(0, 0)
            with eng.Fori(1, CHUNKS - 1) as u:
                a_unit(u, 0)
            a_unit(CHUNKS - 1, 0)
            N = CHUNKS
            iteration(None, 0, None, 0, 0, 0, 1, 0, N)
            iteration(0, 0, None, 0, 1, 0, 2, 0, N + 1)
            iteration(1, 0, 0, 0, 2, 0, 3, 0, N + 2)
            iteration(2, 0, 1, 0, 3, 0, N, 1, N + 3)
            iteration(N - 1, 0, N - 2, 0, N, 1, N + 1, 1, None)
            if eng is nc.vector:
                eng.wait_ge(pvp_done, p_sums(N))
            if eng is nc.gpsimd:
                eng.wait_ge(pvv_done, v_sums(N))
            iteration(N, 1, N - 1, 0, N + 1, 1, N + 2, 1, None)
            iteration(N + 1, 1, N, 1, N + 2, 1, N + 3, 1, None)
            iteration(N + 2, 1, N + 1, 1, N + 3, 1, None, 1, None)
            iteration(N + 3, 1, N + 2, 1, None, 1, None, 1, None)

        assert CHUNKS == 4 and BATCH == 2

        def qk_slot(ring, room, m, nb):
            S = len(ring)
            return room[m] if nb and m < S else ring[m % S]

        def pv_slot(ring, room, m, b):
            S = len(ring)
            return room[m % S] if b else ring[m % S]

        def p_sums(units):
            return PAIRS * min(units, CHUNKS - 1) + SINGLES * max(units - CHUNKS + 1, 0)

        def v_sums(units):
            return len(PV_V[0]) * min(units, CHUNKS - 1) + len(PV_V[1]) * max(units - CHUNKS + 1, 0)

        def last_in_slot(slot, slots, products):
            return max(m for m in range(products) if m % slots == slot) + 1

        def single(u):
            return int(u >= CHUNKS - 1)

        def after_pv(eng, S, m, units, pv_used):
            if S == VSLOTS:
                eng.wait_ge(pv_used, v_sums(units - 1) + last_in_slot(m, S, len(PV_V[single(units - 1)])))
            else:
                eng.wait_ge(pv_used, p_sums(units))

        def qk_slot_free(eng, S, m, n, nb, qk_used, pv_used, other_qk_done):
            T = 2 * S
            if not nb:
                if m >= S or n == 1:
                    eng.wait_ge(qk_used, T * n + m - S + 1)
                elif n > 1:
                    after_pv(eng, S, m, n - 1, pv_used)
            elif n == CHUNKS and m < S:
                eng.wait_ge(other_qk_done, T_OTHER[S] * CHUNKS)
            elif n <= CHUNKS + 1 and m >= S:
                after_pv(eng, S, m - S, n - 1, pv_used)
            else:
                eng.wait_ge(qk_used, T * (n - 1) + m + 1)

        def pv_slot_free(eng, S, m, u, b, qk_used, pv_used):
            T = 2 * S
            if not b and m < S:
                eng.wait_ge(qk_used, T * (u + 2) + m - S + 1)
            elif m >= S:
                eng.wait_ge(pv_used, v_sums(u) + m - S + 1)
            elif u > CHUNKS:
                eng.wait_ge(pv_used, v_sums(u - 1) + last_in_slot(m, S, len(PV_V[1])))

        T_OTHER = {VSLOTS: PBURST, PSLOTS: VBURST}

        def a_base(u, b):
            return 8 * u

        def a_end():
            return a_base(UNITS, 1)

        block = ctx.enter_context(nc.Block())

        @block.sync
        def _(sp):
            def chunk_of(t, u):
                return t[u // CHUNKS, :, CT * (u % CHUNKS):CT * (u % CHUNKS) + CT, :]

            def load_xa(u):
                need(sp, xhatA_done, u)
                sp.dma_start(xa[:, :, :], chunk_of(x_v, u)).then_inc(xa_in, 16)

            def load_xb(u):
                need(sp, y_read, 2 * u)
                sp.dma_start(xb[:, :, :], chunk_of(x_v, u)).then_inc(xb_in, 16)

            def prefix_values(b):
                sp.wait_ge(a_read, a_base(CHUNKS * (b + 1), b) - 2)
                tail = vals[b][:, (PRE + 8) * D:(PRE + TILES) * D]
                sp.dma_start(vals[b][1:P, 0:PRE * D], tail[0:P - 1, :]).then_inc(vpre_in, 16)
                sp.dma_start(vals[b][0:1, 0:PRE * D], tail[P - 1:P, :]).then_inc(vpre_in, 16)

            def store(u):
                sp.wait_ge(y2_read, 2 * u + 2)
                sp.dma_start(chunk_of(out_v, u), xhatC_of(u)[:, :, :]).then_inc(outC_of(u)[0], 16)

            def store_last():
                for n in range(2):
                    sp.wait_ge(y2_read, 2 * LAST + n + 1)
                    sp.dma_start(chunk_of(out_v, LAST)[:, 2 * n:2 * n + 2, :], xhatC_of(LAST)[:, 2 * n:2 * n + 2, :])\
                        .then_inc(outC_of(LAST)[0], 16)

            wmod_v = wmod.rearrange("(k p) n -> p k n", p=P)
            load_xa(0)
            for dst, src in ((cT_sb[:, :, :], cT), (wmod_sb[:, :, 0:2 * D], wmod_v[:, :, 0:2 * D])):
                sp.dma_start(dst, src).then_inc(ld_mod, 16)
            sp.dma_start(circ_sb[:, :], circ).then_inc(ld_circ, 16)
            sp.dma_start(wmod_sb[:, :, 2 * D:6 * D], wmod_v[:, :, 2 * D:6 * D]).then_inc(ld_rest, 16)
            for dst, src in ((wqkv_sb[:, :, :], wqkv.rearrange("(k p) n -> p k n", p=P)), (bqkv_sb[:, :], bqkv)):
                sp.dma_start(dst, src).then_inc(ld_qkv, 16)
            load_xa(1)
            for dst, src in ((wproj_sb, wproj.rearrange("(k p) n -> p k n", p=P)),
                             (wbase_sb, wbase.rearrange("(k p) n -> p k n", p=P)), (wup_sb, wup),
                             (bproj_sb, bproj.rearrange("(a n) -> a n", a=1).broadcast_to([P, D]))):
                sp.dma_start(dst, src).then_inc(ld_scaled, 16)
            load_xa(2)
            for dst, src in ((sel_sb[:, :, :], sel), (mask_sb[:, :], mask),
                             (maskrow_sb[:, :, :], maskrow),
                             (wdown_sb[:, :, :], wdown.rearrange("(k p) n -> p k n", p=P)),
                             (rb_sb[:, :], rb.rearrange("(a n) -> a n", a=1).broadcast_to([P, E])),
                             (lower_sb[:, :, :], lower)):
                sp.dma_start(dst, src).then_inc(ld_const, 16)
            load_xb(0)
            load_xa(3)
            load_xa(4)
            load_xa(5)
            prefix_values(0)
            for u in range(UNITS):
                if u == CHUNKS - 2:
                    prefix_values(1)
                if u + 6 < UNITS:
                    load_xa(u + 6)
                if u:
                    load_xb(u)
                    store(u - 1)
            store_last()
            sp.wait_ge(out2_done, 16 * (outC_of(LAST - 1)[1] + 1))
            sp.wait_ge(outa_done, 16 * (outC_of(LAST)[1] + 2))

        @block.gpsimd
        def _(pool):
            g = nc.gpsimd

            def scale_weights():
                pool.wait_ge(gates_done, 1)
                pool.wait_ge(ld_scaled, 64)
                for b in range(BATCH):
                    for k in range(HALVES):
                        g.tensor_tensor(wproj_s[b][:, k, :], wproj_sb[:, k, :], gates[:, b, 0, :], ALU.mult)\
                            .then_inc(scaled_done, 1)
                        g.tensor_tensor(wbase_s[b][:, k, :], wbase_sb[:, k, :], gates[:, b, 1, :], ALU.mult)\
                            .then_inc(scaled_done, 1)
                    g.tensor_tensor(wup_s[b][:, :], wup_sb, gates[0:NG + 1, b, 1, :], ALU.mult)\
                        .then_inc(scaled_done, 1)
                    g.tensor_tensor(brow[b][:, :], bproj_sb, gates[:, b, 0, :], ALU.mult)\
                        .then_inc(scaled_done, 1)
                pool.wait_ge(scaled_done, 12)

            def rstd(u, stats, step_sem, per, mv, ve, rst, bias, free, done):
                need(pool, done, 2 * u)
                need(pool, free, u)
                pool.wait_ge(stats, 2 * u + 2)
                link, count = steps(pool, step_sem, per * u)
                link(g.tensor_tensor(ve[:, 0, :], mv[:, 4, :], lnc[:, 0, :], ALU.add))
                link(g.tensor_tensor(ve[:, 1, :], ve[:, 0, :], lnc[:, 1, :], ALU.pow))
                link(g.tensor_tensor(ve[:, 2, :], mv[:, 0, :], ve[:, 1, :], ALU.mult))
                assert count[0] == per
                g.tensor_tensor(rst[:, :], ve[:, 1, :], lnc[:, 2, :], ALU.mult).then_inc(done, 1)
                g.tensor_tensor(bias[:, :], ve[:, 2, :], lnc[:, 3, :], ALU.mult).then_inc(done, 1)

            def rstd_a(u):
                rstd(u, statsA, pa_step, PA_STEPS, mvA, veA, rstdA, biasA, xhatA_done, rstdA_done)

            def rstd_c(u):
                rstd(u, statsC, pc_step, PC_STEPS, mvC, veC, rstdC, biasC, xhatC_done, rstdC_done)

            def qk_products(n, nb, half):
                pool.wait_ge(kpre_done, nb + 1)
                chunk = n - CHUNKS * nb
                for m in range(half * PSLOTS, (half + 1) * PSLOTS):
                    qk_slot_free(pool, PSLOTS, m, n, nb, qkp_used, pvp_used, qkv_done)
                    g.tensor_tensor(qk_slot(pring, kroom[VSLOTS:], m, nb).rearrange("p (h t) -> p h t", h=HALVES),
                                    queriesT[:, :, ds(CW * chunk, CW)],
                                    keysT[nb][:, :, ds(PRE * P - COLS[QK_P[m]] + CW * chunk, CW)], ALU.mult)\
                        .then_inc(qkp_done, 1)

            def pv_half(u, b, j):
                if single(u):
                    pv_singles(u, b, j)
                else:
                    pv_pair(u, b, j)

            def pv_singles(u, b, half):
                if half == 0:
                    pool.wait_ge(vpre_in, 32 * (b + 1))
                    pool.wait_ge(probs_done, u + 1)
                for m in (range(PSLOTS), range(PSLOTS, SINGLES))[half]:
                    if m >= PSLOTS:
                        pool.wait_ge(pvp_used, p_sums(u) + m - PSLOTS + 1)
                    elif not b:
                        pool.wait_ge(qkp_used, PBURST * (u + 2) + m - 1)
                    elif u > CHUNKS:
                        pool.wait_ge(pvp_used, p_sums(u - 1) + last_in_slot(m, PSLOTS, SINGLES))
                    k, = PV_P[1][m]
                    g.tensor_tensor(
                        pv_slot(pring, vroom[VSLOTS:], m, b).rearrange("p (a d) -> p a d", d=DH),
                        probs[:, k, :].unsqueeze(2).broadcast_to([P, CT * HEADS, DH]),
                        vals[b][:, ds((PRE - BACK[k]) * D + CT * D * (u - CHUNKS * b), CT * D)]
                        .rearrange("p (a d) -> p a d", d=DH), ALU.mult).then_inc(pvp_done, 1)

            def pv_pair(u, b, j):
                if j == 0:
                    pool.wait_ge(vpre_in, 32 * (b + 1))
                    pool.wait_ge(probs_done, u + 1)
                chunk = u - CHUNKS * b
                slots = [pring[j], pring[1 - j]]
                for i, k in enumerate(PV_P[0][j]):
                    if j == 0:
                        pool.wait_ge(qkp_used, PBURST * (u + 2) + i - 1)
                    elif i == 0:
                        pool.wait_ge(pvp_done, PAIRS * u + 1)
                    else:
                        pool.wait_ge(pvp_used, PAIRS * u + 1)
                    g.tensor_tensor(
                        slots[i].rearrange("p (a d) -> p a d", d=DH),
                        probs[:, k, :].unsqueeze(2).broadcast_to([P, CT * HEADS, DH]),
                        vals[b][:, ds((PRE - BACK[k]) * D + CT * D * chunk, CT * D)]
                        .rearrange("p (a d) -> p a d", d=DH), ALU.mult).then_inc(pair_step, 1)
                pool.wait_ge(pair_step, 4 * u + 2 * j + 2)
                g.tensor_tensor(slots[0], slots[0], slots[1], ALU.add).then_inc(pvp_done, 1)

            def bias_x(u, b):
                pool.wait_ge(xb_in, 16 * u + 16)
                g.tensor_tensor(xb[:, :, :], xb[:, :, :], brow[b][:, :].unsqueeze(1).broadcast_to([P, CT, D]),
                                ALU.add).then_inc(xb_pre, 1)

            def a_unit(u, b):
                if not (isinstance(u, int) and u == CHUNKS - 1):
                    rstd_a(u + 2)

            def iteration(u, b, c, cb, n, nb, m, mb, a):
                if u is None:
                    qk_products(n, nb, 0)
                if a is not None:
                    qk_products(n, nb, 1)
                    if c is not None:
                        rstd_c(c)
                    if u is not None:
                        pv_half(u, b, 0)
                        pv_half(u, b, 1)
                    else:
                        rstd_a(a + 1)
                else:
                    if u == CHUNKS - 1:
                        rstd_c(c)
                    pv_half(u, b, 0)
                    if u != CHUNKS - 1 and n is not None:
                        rstd_c(c)
                    if m is not None:
                        qk_products(m, mb, 0)
                    pv_half(u, b, 1)
                    if n is None:
                        rstd_c(c)
                    bias_x(u, b)
                if a is not None:
                    qk_products(m, mb, 0)
                if a is not None and u is not None:
                    if a < UNITS - 1:
                        rstd_a(a + 1)
                    bias_x(u, b)
                if m is not None and mb:
                    qk_products(m, mb, 1)
                if a is None and n is not None:
                    for i in range(2):
                        pool.wait_ge(y2_out, 2 * (c - CHUNKS + 2) + i + 1)
                        part = xhatC_of(c)[:, 2 * i:2 * i + 2, :]
                        g.tensor_tensor(part, part, x_of(c)[:, 2 * i:2 * i + 2, :], ALU.add).then_inc(y2_read, 1)
                if n is None:
                    rstd_c(u)

            for k, value in enumerate((D * EPS, -0.5, D ** 0.5, -0.5 * D ** 0.5)):
                g.memset(lnc[:, k, :], value).then_inc(const_done, 1)
            g.memset(lora[:, :, NG:NG + 1], 1.0).then_inc(const_done, 1)
            g.memset(keysT[0][:, :, (PRE - 1) * P:PRE * P], 0.0).then_inc(const_done, 1)
            pool.wait_ge(const_done, 6)
            rstd_a(0)
            rstd_a(1)
            schedule(pool, a_unit, scale_weights, iteration)

        @block.scalar
        def _(act):
            s = nc.scalar

            def normalise(u, x_buf, xhat, rst, bias, ready, done):
                act.wait_ge(ready, 2 * u + 2)
                for t in range(CT):
                    ins = s.activation(xhat[:, t, :], x_buf[:, t, :], ACT.Identity,
                                       bias=bias[:, t:t + 1], scale=rst[:, t:t + 1])
                ins.then_inc(done, 1)

            def normalise_a(u, before):
                need(act, a_full, before)
                normalise(u, xa, xhatA, rstdA, biasA, rstdA_done, xhatA_done)

            def normalise_c(u):
                need(act, outC_of(u)[0], 16 * outC_of(u)[1])
                need(act, h2T_full, 2 * u)
                normalise(u, x_of(u), xhatC_of(u), rstdC, biasC, rstdC_done, xhatC_done)

            def evac_a(u, b, group, dst, bank_n, func=ACT.Identity, **kw):
                act.wait_ge(a_full, a_base(u, b) + group + 1)
                s.activation(dst, pA[bank_n][:, :], func, **kw).then_inc(a_read, 1)

            def hT_halves(a, ab):
                for k in range(HALVES):
                    evac_a(a, ab, k, hT[:, k, :], k, bias=modT[:, 0, k, ab:ab + 1],
                           scale=modT[:, 1, k, ab:ab + 1])

            def keys(a, ab):
                for k in range(HALVES):
                    evac_a(a, ab, 2 + k, keysT[ab][:, k, ds(PRE * P + CW * (a - CHUNKS * ab), CW)], k,
                           bias=bqkv_sb[:, 2 + k:3 + k])

            def queries(a, ab, k):
                if ab and k == 0:
                    act.wait_ge(qkv_done, VBURST * (a - CHUNKS + 1))
                    act.wait_ge(qkp_done, PBURST * (a - CHUNKS + 1))
                evac_a(a, ab, 6 + k, queriesT[:, k, ds(CW * (a - CHUNKS * ab), CW)], k, bias=bqkv_sb[:, k:k + 1])

            def values(a, ab, n):
                evac_a(a, ab, 4 + n, vals[ab][:, ds((PRE + 2 * n) * D + CT * D * (a - CHUNKS * ab), 2 * D)], n,
                       ACT.Copy)

            def prefix_keys(b):
                act.wait_ge(a_read, a_base(CHUNKS * (b + 1) - 1, b) + 4)
                if b == 0:
                    act.wait_ge(qkv_done, VSLOTS)
                s.activation(keysT[b][:, :, 0:PRE * P], keysT[b][:, :, (TILES * P - 1):(TILES + PRE) * P - 1],
                             ACT.Copy).then_inc(kpre_done, 1)

            def scores_out(n):
                act.wait_ge(qkv_used, VBURST * (n + 1))
                act.wait_ge(qkp_used, PBURST * (n + 1))
                for k in range(HALVES):
                    s.activation(scoresT[:, k, :], pS[k][:, :], ACT.Copy).then_inc(sT_read, 1)

            def exponentials(u):
                act.wait_ge(ssub_done, 2 * u + 2)
                s.activation(probs[:, :, :], probs[:, :, :], ACT.Exp, scale=SCALE).then_inc(exp_done, 1)

            def h2T_halves(c, cb):
                for k in range(HALVES):
                    act.wait_ge(h2T_full, 2 * c + k + 1)
                    s.activation(h2T_of(c)[:, k, :], sumC(c)[k][:, :], ACT.Identity, bias=modT[:, 2, k, cb:cb + 1],
                                 scale=modT[:, 3, k, cb:cb + 1]).then_inc(h2T_read, 1)

            def router_exp(c):
                act.wait_ge(lsub_done, c + 1)
                s.activation(lexp[:, :, :], lsub[:, :, :], ACT.Exp).then_inc(lexp_done, 1)

            def lora_out(c):
                act.wait_ge(loraT_full, c + 1)
                s.activation(loraT[:, :], downC(c)[1][0:NG + 1, :], ACT.Copy).then_inc(loraT_read, 1)

            def attention_out(u):
                act.wait_ge(pvv_used, v_sums(u + 1))
                act.wait_ge(pvp_used, p_sums(u + 1))
                for k in range(HALVES):
                    s.activation(attnT[:, k, :], pO[k][:, :], ACT.Identity,
                                 bias=bqkv_sb[:, 4 + k:5 + k]).then_inc(attnT_read, 1)

            def shifted_probs(n):
                act.wait_ge(pshift_full, n + 1)
                need(act, pvv_done, v_sums(n))
                s.activation(shifted[:, :, :].rearrange("p k g -> p (k g)"), pA[1][:, 0:NSH * CT * HEADS],
                             ACT.Copy).then_inc(shifted_done, 1)

            def a_unit(u, b):
                hT_halves(u, b)
                keys(u, b)
                normalise_a(u + 1, a_base(u, b) + 2)
                values(u, b, 0)
                values(u, b, 1)
                if isinstance(u, int) and u == CHUNKS - 1:
                    prefix_keys(0)
                queries(u, b, 0)
                queries(u, b, 1)

            def iteration(u, b, c, cb, n, nb, m, mb, a):
                if u is None:
                    act.wait_ge(modT_done, 4)
                    act.wait_ge(scaled_done, 12)
                if a is not None:
                    hT_halves(a, 1)
                    if c is not None:
                        normalise_c(c)
                    keys(a, 1)
                    scores_out(n)
                    if c is not None:
                        h2T_halves(c, cb)
                    values(a, 1, 0)
                    if c is not None:
                        router_exp(c)
                    values(a, 1, 1)
                    if a == UNITS - 1:
                        prefix_keys(1)
                    if c is not None:
                        lora_out(c)
                    exponentials(n)
                    if u is not None:
                        attention_out(u)
                    queries(a, 1, 0)
                    if a < UNITS - 1:
                        normalise_a(a + 1, a_base(a, 1) + 2)
                    if u is None:
                        queries(a, 1, 1)
                    shifted_probs(n)
                    if u is not None:
                        queries(a, 1, 1)
                elif n is not None:
                    normalise_c(c)
                    scores_out(n)
                    h2T_halves(c, cb)
                    router_exp(c)
                    lora_out(c)
                    exponentials(n)
                    attention_out(u)
                    for i in range(2):
                        act.wait_ge(y2_full, 2 * c + i + 1)
                        s.activation(xhatC_of(c)[:, 2 * i:2 * i + 2, :],
                                     sumC(c)[i][:, :].rearrange("p (t c) -> p t c", c=D), ACT.Copy)\
                            .then_inc(y2_out, 1)
                    shifted_probs(n)
                else:
                    normalise_c(c)
                    attention_out(u)
                    h2T_halves(c, cb)
                    router_exp(c)
                    normalise_c(u)
                    h2T_halves(u, b)
                    lora_out(c)
                    router_exp(u)
                    lora_out(u)

            act.wait_ge(ld_mod, 32)
            s.activation(silu[:, 0, :, :], cT_sb[:, :, :], ACT.Exp, scale=-1.0).then_inc(expc_done, 1)
            normalise_a(0, 0)
            act.wait_ge(modT_done, 2)
            act.wait_ge(ld_qkv, 32)
            schedule(act, a_unit, lambda: None, iteration)

        @block.vector
        def _(dve):
            v = nc.vector

            def modulation():
                link, _ = steps(dve, setup_v, 0)
                dve.wait_ge(expc_done, 1)
                link(v.tensor_scalar(silu[:, 1, :, :], silu[:, 0, :, :], 1.0, None, ALU.add))
                link(v.reciprocal(silu[:, 2, :, :], silu[:, 1, :, :]))
                link(v.tensor_tensor(silu[:, 0, :, :], cT_sb[:, :, :], silu[:, 2, :, :], ALU.mult))
                v.tensor_copy(silub, silu[:, 0, :, :].unsqueeze(3).broadcast_to([P, HALVES, BATCH, P]))\
                    .then_inc(silu_done, 1)

            def shift_scale(v_):
                dve.wait_ge(mod_full, v_ + 1)
                src = pO[0][:, 8 * v_:8 * v_ + 8].rearrange("p (s k b) -> p s k b", s=2, k=HALVES)
                v.tensor_copy(modT[:, 2 * v_, :, :], src[:, 0, :, :]).then_inc(modT_done, 1)
                v.tensor_scalar(modT[:, 2 * v_ + 1, :, :], src[:, 1, :, :], 1.0, None, ALU.add)\
                    .then_inc(modT_done, 1)

            def gate_rows():
                link, _ = steps(dve, setup_v, 3)
                for b in range(BATCH):
                    src = pS[b][:, :].rearrange("p (v n) -> p v n", v=2)
                    link(v.tensor_scalar(gsign[:, b, :, :], src, 0.0, 2.0, ALU.is_ge, ALU.mult))
                    link(v.scalar_tensor_tensor(gates[:, b, :, :], gsign[:, b, :, :], -1.0, src, ALU.add,
                                                ALU.mult))
                    link(v.tensor_scalar(gates[:, b, :, :], gates[:, b, :, :], 0.25, None, ALU.max))
                v.scalar_tensor_tensor(gates, gsign, -1.0, gates, ALU.add, ALU.mult).then_inc(gates_done, 1)

            def stats(u, x_buf, bn, mv, step_sem, base, free, done):
                need(dve, free, 2 * u)
                for t in range(CT):
                    v.bn_stats(bn[:, t, :], x_buf[:, t, :]).then_inc(step_sem, 1)
                dve.wait_ge(step_sem, base + CT)
                v.tensor_tensor(mv[:, 0, :], bn[:, :, 1], bn[:, :, 4], ALU.add).then_inc(done, 1)
                v.tensor_tensor(mv[:, 1, :], bn[:, :, 2], bn[:, :, 5], ALU.add).then_inc(step_sem, 1)
                v.tensor_tensor(mv[:, 2, :], bn[:, :, 1], bn[:, :, 4], ALU.subtract).then_inc(step_sem, 1)
                dve.wait_ge(step_sem, base + CT + 2)
                v.scalar_tensor_tensor(mv[:, 3, :], mv[:, 2, :], D / 4, mv[:, 2, :], ALU.mult, ALU.mult)\
                    .then_inc(step_sem, 1)
                dve.wait_ge(step_sem, base + CT + 3)
                v.tensor_tensor(mv[:, 4, :], mv[:, 1, :], mv[:, 3, :], ALU.add).then_inc(done, 1)

            def stats_a(u):
                dve.wait_ge(xa_in, 16 * u + 16)
                stats(u, xa, bnA, mvA, va_step, VA_STEPS * u, rstdA_done, statsA)

            def residual_a(u):
                dve.wait_ge(xb_pre, u + 1)
                if u == 1 or u >= CHUNKS:
                    dve.wait_ge(y2_read, 2 * (u if u == 1 else u - 1))
                bank, x_buf = pB if u < CHUNKS - 1 else pA, x_of(u)
                for n in range(2):
                    dve.wait_ge(y_full, 2 * u + n + 1)
                    v.tensor_tensor(x_buf[:, 2 * n:2 * n + 2, :], bank[n][:, :].rearrange("p (t c) -> p t c", c=D),
                                    xb[:, 2 * n:2 * n + 2, :], ALU.add).then_inc(y_read, 1)
                dve.wait_ge(y_read, 2 * u + 2)
                stats(u, x_buf, bnC, mvC, vc_step, VC_STEPS * u, rstdC_done, statsC)

            def qk_products(n, nb, half):
                if n == 0 and half == 0:
                    dve.wait_ge(a_read, 8)
                    dve.wait_ge(const_done, 6)
                    dve.wait_ge(gates_done, 1)
                else:
                    dve.wait_ge(kpre_done, nb + 1)
                chunk = n - CHUNKS * nb
                for m in range(half * VSLOTS, (half + 1) * VSLOTS):
                    qk_slot_free(dve, VSLOTS, m, n, nb, qkv_used, pvv_used, qkp_done)
                    v.tensor_tensor(qk_slot(vring, kroom, m, nb).rearrange("p (h t) -> p h t", h=HALVES),
                                    queriesT[:, :, ds(CW * chunk, CW)],
                                    keysT[nb][:, :, ds(PRE * P - COLS[QK_V[m]] + CW * chunk, CW)], ALU.mult)\
                        .then_inc(qkv_done, 1)

            def pv_products(u, b, half):
                if half == 0:
                    dve.wait_ge(vpre_in, 32 * (b + 1))
                chunk = u - CHUNKS * b
                mine = PV_V[single(u)]
                for m in range(half * VSLOTS, min((half + 1) * VSLOTS, len(mine))):
                    k = mine[m]
                    pv_slot_free(dve, VSLOTS, m, u, b, qkv_used, pvv_used)
                    if k == 1:
                        dve.wait_ge(shifted_done, u + 1)
                    pr = probs[:, k, :] if k == 0 else shifted[:, k - 1, :]
                    v.tensor_tensor(
                        pv_slot(vring, vroom, m, b).rearrange("p (a d) -> p a d", d=DH),
                        pr.unsqueeze(2).broadcast_to([P, CT * HEADS, DH]),
                        vals[b][:, ds((PRE - BACK[k]) * D + CT * D * chunk, CT * D)]
                        .rearrange("p (a d) -> p a d", d=DH), ALU.mult).then_inc(pvv_done, 1)

            def softmax_front(u):
                need(dve, pvp_done, p_sums(u))
                need(dve, pshift_full, u)
                link, count = steps(dve, vb_step, VB_STEPS * u)
                mx, mx1 = (t[:, :].rearrange("p (g h) -> p g h", h=HH) for t in (smax, srec))
                G = CT * HALVES
                part = []
                for i, most in enumerate((mx, mx1)):
                    dve.wait_ge(stok_full, 2 * u + i + 1)
                    if i == 0:
                        sc = pS[0][:, :].rearrange("p (g o h) -> p g o h", g=G, o=8)
                    else:
                        sc = pS[1][:, :].rearrange("p (g o w h) -> p g o w h", g=G, o=4, w=2)[:, :, :, 0, :]
                    part.append(sc)
                    link(v.tensor_reduce(most, sc.rearrange("p g o h -> p g h o"), AX.X, ALU.max))
                link(v.tensor_tensor(mx, mx, mx1, ALU.max))
                for i, (first, n) in enumerate(((0, 8), (8, 4))):
                    v.tensor_tensor(
                        probs[:, first:first + n, :].rearrange("p o (g h) -> p g o h", h=HH), part[i],
                        mx.unsqueeze(2).broadcast_to([P, G, n, HH]), ALU.subtract).then_inc(ssub_done, 1)
                assert count[0] == 3

            def softmax_back(u):
                link, count = steps(dve, vb_step, VB_STEPS * u + 3)
                dve.wait_ge(exp_done, u + 1)
                link(v.tensor_reduce(ssum[:, :], probs[:, :, :].rearrange("p o g -> p g o"), AX.X, ALU.add))
                link(v.reciprocal(srec[:, :], ssum[:, :]))
                v.tensor_tensor(probs[:, :, :], probs[:, :, :],
                                srec[:, :].unsqueeze(1).broadcast_to([P, ND, CT * HEADS]), ALU.mult)\
                    .then_inc(probs_done, 1)
                dve.wait_ge(probs_done, u + 1)
                assert count[0] == 2

            def router(u):
                link, count = steps(dve, vr_step, VR_STEPS * u)
                dve.wait_ge(down_full, u + 1)
                down = downC(u)[0][:, 0:CT * NA].rearrange("p (t n) -> p t n", n=NA)
                link(v.tensor_tensor(lg[:, :, :], down[:, :, NG:NA],
                                     rb_sb[:, :].unsqueeze(1).broadcast_to([P, CT, E]), ALU.add))
                link(v.tensor_reduce(lmax[:, :], lg[:, :, :], AX.X, ALU.max))
                v.tensor_tensor(lsub[:, :, :], lg[:, :, :], lmax[:, :].unsqueeze(2).broadcast_to([P, CT, E]),
                                ALU.subtract).then_inc(lsub_done, 1)
                other = lg[:, :, :].unsqueeze(2).broadcast_to([P, CT, E, E])
                own = lg[:, :, :].unsqueeze(3).broadcast_to([P, CT, E, E])
                link(v.tensor_tensor(level[:, :, :, :], other, own, ALU.is_ge))
                link(v.tensor_tensor(above[:, :, :, :], other, own, ALU.is_gt))
                link(v.tensor_tensor(level[:, :, :, :], level[:, :, :, :],
                                     lower_sb[:, :, :].unsqueeze(1).broadcast_to([P, CT, E, E]), ALU.mult))
                link(v.tensor_tensor(above[:, :, :, :], above[:, :, :, :], level[:, :, :, :], ALU.max))
                link(v.tensor_reduce(rank[:, :, :], above[:, :, :, :], AX.X, ALU.add))
                dve.wait_ge(lexp_done, u + 1)
                link(v.scalar_tensor_tensor(picked[:, :, :], rank[:, :, :], TOPK - 0.5, lexp[:, :, :],
                                            ALU.is_lt, ALU.mult))
                link(v.tensor_reduce(zall[:, :], lexp[:, :, :], AX.X, ALU.add))
                link(v.tensor_reduce(zpick[:, :], picked[:, :, :], AX.X, ALU.add))
                link(v.scalar_tensor_tensor(zall[:, :], zall[:, :], 1e-6, zpick[:, :], ALU.mult, ALU.add))
                link(v.reciprocal(zrec[:, :], zall[:, :]))
                link(v.tensor_tensor(wsel[:, :, :], picked[:, :, :],
                                     zrec[:, :].unsqueeze(2).broadcast_to([P, CT, E]), ALU.mult))
                need(dve, loraT_full, u)
                v.tensor_tensor(lora[:, :, 0:NR].rearrange("p t (e r) -> p t e r", r=R),
                                down[:, :, 0:NR].rearrange("p t (e r) -> p t e r", r=R),
                                wsel[:, :, :].unsqueeze(3).broadcast_to([P, CT, E, R]), ALU.mult)\
                    .then_inc(lora_done, 1)
                v.tensor_copy(lora[:, :, NR:NG], down[:, :, NR:NG]).then_inc(lora_done, 1)
                assert count[0] == VR_STEPS

            def residual_c(u):
                for n in range(2):
                    dve.wait_ge(y2_full, 2 * u + n + 1)
                    v.tensor_tensor(xhatC_of(u)[:, 2 * n:2 * n + 2, :],
                                    sumC(u)[n][:, :].rearrange("p (t c) -> p t c", c=D),
                                    x_of(u)[:, 2 * n:2 * n + 2, :], ALU.add).then_inc(y2_read, 1)

            def a_unit(u, b):
                if isinstance(u, int) and u == CHUNKS - 1:
                    qk_products(0, 0, 0)
                else:
                    stats_a(u + 2)

            def setup():
                shift_scale(1)
                gate_rows()

            def iteration(u, b, c, cb, n, nb, m, mb, a):
                if a is not None:
                    if c is not None:
                        residual_a(c)
                    qk_products(n, nb, 1)
                    if u is not None:
                        pv_products(u, b, 0)
                    if c is not None:
                        router(c)
                    if u is not None:
                        pv_products(u, b, 1)
                    else:
                        stats_a(a + 1)
                    softmax_front(n)
                    if u is not None and a < UNITS - 1:
                        stats_a(a + 1)
                    softmax_back(n)
                    qk_products(m, mb, 0)
                    if c is not None:
                        residual_c(c)
                    if mb:
                        qk_products(m, mb, 1)
                elif n is not None:
                    residual_a(c)
                    pv_products(u, b, 0)
                    if m is not None:
                        qk_products(m, mb, 0)
                    pv_products(u, b, 1)
                    router(c)
                    softmax_front(n)
                    softmax_back(n)
                    if m is not None:
                        qk_products(m, mb, 1)
                else:
                    pv_products(u, b, 0)
                    residual_a(c)
                    pv_products(u, b, 1)
                    residual_a(u)
                    router(c)
                    router(u)
                    residual_c(c)
                    residual_c(u)

            stats_a(0)
            modulation()
            shift_scale(0)
            stats_a(1)
            schedule(dve, a_unit, setup, iteration)

        @block.tensor
        def _(pe):
            t_ = nc.tensor
            ident = circ_sb[:, 0:P]

            def a_group(u, b, group):
                need(pe, a_read, a_base(u, b) + group - 1)
                if b and (u, group) == (CHUNKS + 1, 1) or b and u > CHUNKS and group == 7:
                    pe.wait_ge(shifted_done, u - CHUNKS + group // 7)
                return pA[group % 2]

            def hT_transposes(a, ab):
                pe.wait_ge(xhatA_done, a + 1)
                for k in range(HALVES):
                    dst = a_group(a, ab, k)
                    for t in range(CT):
                        ins = t_.transpose(dst[:, t * P:(t + 1) * P], xhatA[:, t, k * P:(k + 1) * P], ident)
                    ins.then_inc(a_full, 1)

            def project_T(a, ab, group, col):
                dst = a_group(a, ab, group)
                for k in range(HALVES):
                    if group == 2:
                        pe.wait_ge(a_read, a_base(a, ab) + k + 1)
                    ins = t_.matmul(dst[:, :], wqkv_sb[:, k, col:col + P], hT[:, k, :], start=(k == 0),
                                    stop=(k == HALVES - 1))
                ins.then_inc(a_full, 1)

            def keys(a, ab):
                for k in range(HALVES):
                    project_T(a, ab, 2 + k, D + k * P)

            def queries(a, ab, k):
                project_T(a, ab, 6 + k, k * P)

            def values(a, ab, n):
                dst = a_group(a, ab, 4 + n)
                for t in range(2):
                    for k in range(HALVES):
                        col = (2 * n + t) * P
                        ins = t_.matmul(dst[:, t * D:(t + 1) * D], hT[:, k, col:col + P],
                                        wqkv_sb[:, k, 2 * D:3 * D], start=(k == 0), stop=(k == HALVES - 1))
                ins.then_inc(a_full, 1)

            START_ROUND = (0, 1)

            def scores(n, nb, rounds):
                chunk = n - CHUNKS * nb
                for r in rounds:
                    if r == START_ROUND[n == 0]:
                        need(pe, ssub_done, 2 * n)
                        for i in range(2):
                            t_.matmul(pS[i][:, :], maskrow_sb[:, i, :], mask_sb[:, ds(CW * chunk, CW)],
                                      start=True, stop=False, skip_group_check=True)
                    e, ks = QK_ROUNDS[r]
                    count = sum(len(k) for w, k in QK_ROUNDS[:r + 1] if w == e)
                    if e == "v":
                        pe.wait_ge(qkv_done, VBURST * n + count)
                    else:
                        pe.wait_ge(qkp_done, PBURST * n + count)
                    for h in range(HALVES):
                        for i, k in enumerate(ks):
                            src = (qk_slot(vring, kroom, QK_V.index(k), nb) if e == "v" else
                                   qk_slot(pring, kroom[VSLOTS:], QK_P.index(k), nb))
                            at = 64 * h + 32 * i
                            rows = k % 4 if e == "v" else 2 * (k % 2)
                            ins = t_.matmul(pS[k // 8][at:at + 32, :], sel_sb[:, rows, :],
                                            src[:, h * CW:(h + 1) * CW], start=False,
                                            stop=(k in (3, 7, 9, 11)), skip_group_check=True)
                            if h == HALVES - 1:
                                ins.then_inc(qkv_used if e == "v" else qkp_used, 1)

            def score_transposes(n):
                pe.wait_ge(sT_read, 2 * n + 2)
                for i in range(2):
                    for t in range(CT):
                        ins = t_.transpose(pS[i][:, t * P:(t + 1) * P], scoresT[:, i, t * P:(t + 1) * P], ident)
                    ins.then_inc(stok_full, 1)

            def shift_probs(n, a):
                if a is not None:
                    pe.wait_ge(a_read, a_base(a, 1) + (8 if a == CHUNKS else 6))
                else:
                    pe.wait_ge(a_read, a_end())
                    pe.wait_ge(y_read, 2 * n - 2)
                pe.wait_ge(probs_done, n + 1)
                for k in range(1, 1 + NSH):
                    ins = t_.matmul(pA[1][:, (k - 1) * CT * HEADS:k * CT * HEADS], circ_sb[:, SHIFT[k]:SHIFT[k] + P],
                                    probs[:, k, :], start=True, stop=True)
                ins.then_inc(pshift_full, 1)

            def attend(u, b, first, last):
                if first == 0:
                    need(pe, attnT_read, 2 * u)
                for i, (e, k) in list(enumerate(PV_ORDER[single(u)]))[first:last]:
                    if e == "v":
                        m = PV_V[single(u)].index(k)
                        src = pv_slot(vring, vroom, m, b)
                        pe.wait_ge(pvv_done, v_sums(u) + m + 1)
                    else:
                        m = PV_P[single(u)].index(k)
                        src = pv_slot(pring, vroom[VSLOTS:], m, b)
                        pe.wait_ge(pvp_done, p_sums(u) + m + 1)
                    shift = SHIFT[k] if e == "v" else 0
                    place = circ_sb[:, P - shift:2 * P - shift]
                    for t in range(CT):
                        for h in range(HALVES):
                            at = t * D + h * P
                            ins = t_.matmul(pO[h][:, t * P:(t + 1) * P], src[:, at:at + P], place,
                                            start=(i == 0 and t == 0), stop=(i == len(PV_ORDER[single(u)]) - 1),
                                            is_transpose=True, skip_group_check=True)
                    ins.then_inc(pvv_used if e == "v" else pvp_used, 1)

            def project(u, b, n_next, a):
                pe.wait_ge(attnT_read, 2 * u + 2)
                dst = pB
                if a is None:
                    dst = pA
                    pe.wait_ge(a_read, a_end())
                    pe.wait_ge(y_read, 2 * u)
                for n in range(2):
                    if a is None and n == 1 and n_next is not None:
                        pe.wait_ge(shifted_done, n_next + 1)
                    if a is not None:
                        need(pe, y2_read, 2 * u - 1 + n)
                    for t in range(2):
                        for k in range(HALVES):
                            col = (2 * n + t) * P
                            ins = t_.matmul(dst[n][:, t * D:(t + 1) * D], attnT[:, k, col:col + P],
                                            wproj_s[b][:, k, :], start=(k == 0), stop=(k == HALVES - 1))
                    ins.then_inc(y_full, 1)

            def h2T_transposes(c):
                pe.wait_ge(xhatC_done, c + 1)
                if c != LAST:
                    need(pe, y2_read, 2 * c)
                for k in range(HALVES):
                    pe.wait_ge(y_read, 2 * c + 1 + k)
                    for t in range(CT):
                        ins = t_.transpose(sumC(c)[k][:, t * P:(t + 1) * P],
                                           xhatC_of(c)[:, t, k * P:(k + 1) * P], ident)
                    ins.then_inc(h2T_full, 1)

            def down(c):
                pe.wait_ge(h2T_read, 2 * c + 2)
                for t in range(CT):
                    for k in range(HALVES):
                        ins = t_.matmul(downC(c)[0][:, t * NA:(t + 1) * NA], h2T_of(c)[:, k, t * P:(t + 1) * P],
                                        wdown_sb[:, k, :], start=(k == 0), stop=(k == HALVES - 1))
                ins.then_inc(down_full, 1)

            def lora_transposes(c):
                pe.wait_ge(lora_done, 2 * c + 2)
                for t in range(CT):
                    ins = t_.transpose(downC(c)[1][0:NG + 1, t * P:(t + 1) * P], lora[:, t, :], ident)
                ins.then_inc(loraT_full, 1)

            def up(c, cb, base=True, ranks=True):
                if ranks:
                    pe.wait_ge(loraT_read, c + 1)
                for n in range(2):
                    if base and c == LAST:
                        pe.wait_ge(h2T_read, 2 * c + 2)
                    for t in range(2):
                        col = (2 * n + t) * P
                        dst = sumC(c)[n][:, t * D:(t + 1) * D]
                        for k in range(HALVES):
                            if base:
                                t_.matmul(dst, h2T_of(c)[:, k, col:col + P], wbase_s[cb][:, k, :],
                                          start=(k == 0 and (ranks or t == 0)), stop=False,
                                          skip_group_check=True)
                        if ranks:
                            ins = t_.matmul(dst, loraT[:, col:col + P], wup_s[cb][:, :], start=False, stop=True,
                                            skip_group_check=True)
                    if ranks:
                        ins.then_inc(y2_full, 1)

            def a_unit(u, b):
                if isinstance(u, int) and u == 0:
                    pe.wait_ge(ld_circ, 16)
                    hT_transposes(u, b)
                    gates_and_shift()
                    pe.wait_ge(ld_qkv, 32)
                else:
                    hT_transposes(u, b)
                keys(u, b)
                values(u, b, 0)
                values(u, b, 1)
                queries(u, b, 0)
                queries(u, b, 1)

            def iteration(u, b, c, cb, n, nb, m, mb, a):
                if u is None:
                    pe.wait_ge(ld_const, 16 * 6)
                    pe.wait_ge(gates_done, 1)
                    pe.wait_ge(const_done, 6)
                    pe.wait_ge(scaled_done, 12)
                early, middle = (0, 7) if a is not None else (0 if u == CHUNKS - 1 else 3, 11)
                if a is not None:
                    if u is None:
                        scores(n, nb, (1, 2))
                        hT_transposes(a, 1)
                        scores(n, nb, (0,))
                    else:
                        hT_transposes(a, 1)
                        scores(n, nb, range(3))
                    keys(a, 1)
                    scores(n, nb, range(3, 6))
                    if c is not None:
                        h2T_transposes(c)
                    values(a, 1, 0)
                    if c is not None:
                        down(c)
                    score_transposes(n)
                    values(a, 1, 1)
                elif n is not None:
                    scores(n, nb, range(6))
                    attend(u, b, 0, early)
                    h2T_transposes(c)
                    score_transposes(n)
                    down(c)
                else:
                    attend(u, b, 0, len(PV_ORDER[single(u)]))
                    h2T_transposes(c)
                    project(u, b, n, a)
                    down(c)
                    h2T_transposes(u)
                    lora_transposes(c)
                    down(u)
                    up(c, cb)
                    up(u, b, ranks=False)
                    lora_transposes(u)
                    up(u, b, base=False)
                    return
                if u is not None:
                    attend(u, b, early, middle)
                if c is not None:
                    lora_transposes(c)
                if u is not None:
                    attend(u, b, middle, len(PV_ORDER[single(u)]))
                if a is not None:
                    queries(a, 1, 0)
                if c is not None:
                    up(c, cb)
                elif u is not None:
                    project(u, b, n, a)
                if u is None:
                    queries(a, 1, 1)
                shift_probs(n, a)
                if a is not None and u is not None:
                    queries(a, 1, 1)
                if c is not None:
                    project(u, b, n, a)

            def shift_scale(v_):
                for n in range(2):
                    for h in range(HALVES):
                        at = ((2 * v_ + n) * HALVES + h) * BATCH
                        for k in range(HALVES):
                            col = (3 * v_ + n) * D + h * P
                            ins = t_.matmul(pO[0][:, at:at + BATCH], wmod_sb[:, k, col:col + P],
                                            silu[:, 0, k, :], start=(k == 0), stop=(k == 1))
                ins.then_inc(mod_full, 1)

            def gates_and_shift():
                pe.wait_ge(ld_rest, 16)
                for b in range(BATCH):
                    for n, vec in enumerate((2, 5)):
                        for k in range(HALVES):
                            t_.matmul(pS[b][:, n * D:(n + 1) * D], silub[:, k, b, :],
                                      wmod_sb[:, k, vec * D:(vec + 1) * D], start=(k == 0), stop=(k == 1))
                pe.wait_ge(modT_done, 2)
                shift_scale(1)

            pe.wait_ge(silu_done, 1)
            pe.wait_ge(ld_mod, 32)
            shift_scale(0)
            schedule(pe, a_unit, lambda: None, iteration)


def kernel(**inputs):
    import numpy as np
    import concourse.bacc as bacc
    from ml_dtypes import bfloat16 as bf16
    from concourse.bass_utils import run_bass_kernel_spmd

    f = {k.replace("L0_attn_", "").replace("L0_ffn_", "").replace("L0_", ""): np.ascontiguousarray(v)
         for k, v in inputs.items()}
    circ = ((np.arange(2 * P)[None, :] - np.arange(P)[:, None]) % P == 0).astype(np.float32)
    sel = np.zeros((P, 4, 32), np.float32)
    for n in range(4):
        sel[np.arange(P), n, n * HH + np.arange(P) // DH] = 1.0
    token = (np.arange(TILES)[:, None] + TILES * np.arange(P)[None, :]).reshape(-1)
    mask = np.where(token[None, :] < np.array(DIST)[:, None], MASKED, 0.0).astype(bf16)
    maskrow = np.zeros((ND, 2, HALVES, 64), np.float32)
    for k in range(ND):
        at = k * HH if k < 8 else (k - 8) * 2 * HH
        maskrow[k, k // 8, :, at:at + HH] = 1.0
    maskrow = maskrow.reshape(ND, 2, P).astype(bf16)
    lower = np.broadcast_to((np.arange(E)[None, :] < np.arange(E)[:, None]).astype(np.float32), (P, E, E))
    arrays = {
        "x": f["x"],
        "cT": f["c"].T.reshape(HALVES, P, BATCH).transpose(1, 0, 2),
        "wmod": f["wmod"],
        "wqkv": f["W_qkv"],
        "bqkv": f["b_qkv"].reshape(3 * HALVES, P).T,
        "wproj": f["W_proj"],
        "bproj": f["b_proj"],
        "wbase": f["base_W"].T,
        "wdown": np.concatenate([f["routed_A"].reshape(NR, D), f["shared_A"], f["router_W"]]).T,
        "wup": np.concatenate([f["routed_B"].transpose(0, 2, 1).reshape(NR, D), f["shared_B"].T,
                               f["base_b"][None, :]]),
        "rb": f["router_b"],
        "circ": circ, "sel": sel, "mask": mask, "maskrow": maskrow, "lower": lower,
    }
    arrays = {f"in_{k}": np.ascontiguousarray(a) for k, a in arrays.items()}
    nc = bacc.Bacc("TRN2", target_bir_lowering=False, num_devices=1)
    args = [nc.dram_tensor(k, a.shape, mybir.dt.from_np(a.dtype), kind="ExternalInput").ap()
            for k, a in arrays.items()]
    args.append(nc.dram_tensor("out", f["x"].shape, F32, kind="ExternalOutput").ap())
    build(nc, *args)
    r = run_bass_kernel_spmd(nc, [arrays], core_ids=[0])
    return r.results[0]["out"]
```
